# Optimizing a Trainium2 kernel written in Bass

```python
import numpy as np
import jax
import jax.numpy as jnp

def _softmax(x, axis=-1):
    return jax.nn.softmax(x, axis=axis)

def _gelu(x):
    return jax.nn.gelu(x, approximate=True)

def _silu(x):
    return jax.nn.silu(x)

def _sigmoid(x):
    return jax.nn.sigmoid(x)

def _layernorm(x, axis=-1, eps=1e-05):
    m = jnp.mean(x, axis=axis, keepdims=True)
    v = jnp.var(x, axis=axis, keepdims=True)
    return (x - m) / jnp.sqrt(v + eps)

def _scatter_add(tgt, idx, src, axis=0):
    return tgt.at[idx].add(src)

def _segment_sum(src, seg, n):
    return jax.ops.segment_sum(src, seg, n)
kernel_name = 'mk_adaln_attn_ffn_d1_seqx_r4_1d57a6'

def setup_inputs(seed: int=0):
    np.random.seed(seed)
    _w = jnp.asarray

    def _rec_inputs():
        import jax
        import jax.numpy as jnp
        _rk = jax.random.key(seed)
        x = -0.000125 + 0.9999 * jax.random.normal(jax.random.fold_in(_rk, 1), (32, 64, 1024), jnp.float32)
        _lenS = 64 - jax.random.randint(jax.random.fold_in(_rk, 7), (32,), 0, max(1, 64 // 4) + 1, jnp.int32)
        _lenS2 = 64 - jax.random.randint(jax.random.fold_in(_rk, 8), (32,), 0, max(1, 64 // 4) + 1, jnp.int32)
        cond_128 = 0.0061147 + 1.02565 * jax.random.normal(jax.random.fold_in(_rk, 11), (32, 128), jnp.float32)
        fside_S_0 = -0.022604 + 0.987366 * jax.random.normal(jax.random.fold_in(_rk, 12), (64,), jnp.float32)
        return (x, cond_128, fside_S_0)
    x, cond_128, fside_S_0 = _rec_inputs()

    def _L0_cond_setup():
        import jax, jax.numpy as jnp
        import numpy as np
        K = 8
        T = 1.0
        D_EMBD = 128
        IN_C = 64
        OUT_C = 64
        BS = 32
        H = 1024
        HID = 128
        key = jax.random.key(seed)
        ks = jax.random.split(key, 10)
        s = lambda fan_in: 1.0 / np.sqrt(fan_in)
        return {'x': jax.random.normal(ks[0], (BS, IN_C, H), dtype=jnp.float32), 'embedding': jax.random.normal(ks[1], (BS, D_EMBD), dtype=jnp.float32), 'W0': jax.random.normal(ks[2], (D_EMBD, HID), dtype=jnp.float32) * s(D_EMBD), 'b0': jnp.zeros((HID,), dtype=jnp.float32), 'W1': jax.random.normal(ks[3], (HID, HID), dtype=jnp.float32) * s(HID), 'b1': jnp.zeros((HID,), dtype=jnp.float32), 'W2': jax.random.normal(ks[4], (HID, K), dtype=jnp.float32) * s(HID), 'b2': jnp.zeros((K,), dtype=jnp.float32), 'weight': jax.random.normal(ks[5], (K, OUT_C, IN_C, 1), dtype=jnp.float32) * s(IN_C), 'bias_k': jax.random.normal(ks[6], (K, OUT_C), dtype=jnp.float32) * 0.1}
    _L0_cond_all = _L0_cond_setup()
    _L0_cond_in = {k: v for k, v in _L0_cond_all.items() if k in ('W0', 'b0', 'W1', 'b1', 'W2', 'b2', 'weight', 'bias_k')}
    del _L0_cond_all

    def _L0_attn_setup():
        import math
        import jax, jax.numpy as jnp
        import numpy as np
        NUM_HEADS = 32
        HIDDEN = 1024
        HEAD_DIM = HIDDEN // NUM_HEADS
        NEG_INF = -1e+30

        def _alibi_slopes(n: int) -> jnp.ndarray:
            cp2 = 2 ** math.floor(math.log2(n))
            base = 2.0 ** (-2.0 ** (-(math.log2(cp2) - 3)))
            slopes = base ** np.arange(1, cp2 + 1, dtype=np.float64)
            if cp2 != n:
                extra_base = 2.0 ** (-2.0 ** (-(math.log2(2 * cp2) - 3)))
                rem = min(cp2, n - cp2)
                extra = extra_base ** np.arange(1, 1 + 2 * rem, 2, dtype=np.float64)
                slopes = np.concatenate([slopes, extra])
            return jnp.asarray(slopes, dtype=jnp.float32)
        key = jax.random.key(seed)
        k1, k2, k3 = jax.random.split(key, 3)
        B, S = (2, 512)
        hidden_states = jax.random.normal(k1, (B, S, HIDDEN), dtype=jnp.float32)
        Wqkv = jax.random.normal(k2, (HIDDEN, NUM_HEADS * HEAD_DIM + 2 * HEAD_DIM), dtype=jnp.float32) * 0.02
        Wo = jax.random.normal(k3, (HIDDEN, HIDDEN), dtype=jnp.float32) * 0.02
        return {'hidden_states': hidden_states, 'Wqkv': Wqkv, 'Wo': Wo}
    _L0_attn_all = _L0_attn_setup()
    _L0_attn_in = {k: v for k, v in _L0_attn_all.items() if k in ('Wqkv', 'Wo')}
    del _L0_attn_all

    def _L0_cond2_setup():
        import jax, jax.numpy as jnp
        import numpy as np
        from jax import lax
        N, C_IN, L = (32, 64, 1024)
        C_OUT, K, GROUPS = (64, 9, 4)
        C_DIM, PAD, STRIDE = (128, 4, 1)
        key = jax.random.key(seed)
        k1, k2, k3, k4, k5 = jax.random.split(key, 5)
        x = jax.random.normal(k1, (N, C_IN, L), dtype=jnp.float32)
        c = jax.random.normal(k2, (N, C_DIM), dtype=jnp.float32)
        weight = jax.random.normal(k3, (C_OUT, C_IN // GROUPS, K), dtype=jnp.float32)
        c_weight = jax.random.normal(k4, (C_OUT, C_DIM), dtype=jnp.float32)
        bias = jax.random.normal(k5, (C_OUT,), dtype=jnp.float32)
        return {'x': x, 'c': c, 'weight': weight, 'c_weight': c_weight, 'bias': bias}
    _L0_cond2_all = _L0_cond2_setup()
    _L0_cond2_in = {k: v for k, v in _L0_cond2_all.items() if k in ('weight', 'c_weight')}
    del _L0_cond2_all

    def _L0_ffn_setup():
        import jax, jax.numpy as jnp
        import numpy as np
        B, S, IN, OUT = (4, 512, 1024, 1024)
        E, K, R = (8, 2, 16)
        CAP_FACTOR = 3.0
        ALPHA = 1.0 / R
        LN_EPS = 1e-05
        key = jax.random.key(seed)
        ks = jax.random.split(key, 6)
        return {'x': jax.random.normal(ks[0], (B, S, IN), dtype=jnp.float32), 'weight': jax.random.normal(ks[1], (OUT, IN), dtype=jnp.float32) * 0.02, 'lora_A': jax.random.normal(ks[2], (E, IN, R), dtype=jnp.float32) / np.sqrt(R), 'lora_B': jax.random.normal(ks[3], (E, R, OUT), dtype=jnp.float32) * 0.02, 'gw1': jax.random.normal(ks[4], (4 * E, IN), dtype=jnp.float32) * 0.02, 'gb1': jnp.zeros((4 * E,), dtype=jnp.float32), 'ln_gamma': jnp.ones((4 * E,), dtype=jnp.float32), 'ln_beta': jnp.zeros((4 * E,), dtype=jnp.float32), 'gw2': jax.random.normal(ks[5], (E, 4 * E), dtype=jnp.float32) * 0.02, 'gb2': jnp.zeros((E,), dtype=jnp.float32)}
    _L0_ffn_all = _L0_ffn_setup()
    _L0_ffn_in = {k: v for k, v in _L0_ffn_all.items() if k in ('weight', 'lora_A', 'lora_B', 'gw1', 'gb1', 'ln_gamma', 'ln_beta', 'gw2', 'gb2')}
    del _L0_ffn_all
    return {'x': x, 'cond_128': cond_128, 'fside_S_0': fside_S_0, 'L0_cond_W0': _L0_cond_in['W0'], 'L0_cond_b0': _L0_cond_in['b0'], 'L0_cond_W1': _L0_cond_in['W1'], 'L0_cond_b1': _L0_cond_in['b1'], 'L0_cond_W2': _L0_cond_in['W2'], 'L0_cond_b2': _L0_cond_in['b2'], 'L0_cond_weight': _L0_cond_in['weight'], 'L0_cond_bias_k': _L0_cond_in['bias_k'], 'L0_attn_Wqkv': _L0_attn_in['Wqkv'], 'L0_attn_Wo': _L0_attn_in['Wo'], 'L0_cond2_weight': _L0_cond2_in['weight'], 'L0_cond2_c_weight': _L0_cond2_in['c_weight'], 'L0_ffn_weight': _L0_ffn_in['weight'], 'L0_ffn_lora_A': _L0_ffn_in['lora_A'], 'L0_ffn_lora_B': _L0_ffn_in['lora_B'], 'L0_ffn_gw1': _L0_ffn_in['gw1'], 'L0_ffn_gb1': _L0_ffn_in['gb1'], 'L0_ffn_ln_gamma': _L0_ffn_in['ln_gamma'], 'L0_ffn_ln_beta': _L0_ffn_in['ln_beta'], 'L0_ffn_gw2': _L0_ffn_in['gw2'], 'L0_ffn_gb2': _L0_ffn_in['gb2']}

def reference(x, cond_128, fside_S_0, L0_cond_W0, L0_cond_b0, L0_cond_W1, L0_cond_b1, L0_cond_W2, L0_cond_b2, L0_cond_weight, L0_cond_bias_k, L0_attn_Wqkv, L0_attn_Wo, L0_cond2_weight, L0_cond2_c_weight, L0_ffn_weight, L0_ffn_lora_A, L0_ffn_lora_B, L0_ffn_gw1, L0_ffn_gb1, L0_ffn_ln_gamma, L0_ffn_ln_beta, L0_ffn_gw2, L0_ffn_gb2):
    import jax
    import jax.numpy as jnp

    def _L0_cond_ref(x, embedding, W0, b0, W1, b1, W2, b2, weight, bias_k):
        import jax, jax.numpy as jnp
        import numpy as np
        K = 8
        T = 1.0
        D_EMBD = 128
        IN_C = 64
        OUT_C = 64
        BS = 32
        H = 1024
        HID = 128
        h = jax.nn.gelu(embedding @ W0 + b0, approximate=False)
        h = jax.nn.gelu(h @ W1 + b1, approximate=False)
        att = jax.nn.softmax((h @ W2 + b2) / T, axis=-1)
        agg_w = jnp.einsum('bk,koi->boi', att, weight[..., 0])
        agg_b = att @ bias_k
        out = jnp.einsum('boi,bih->boh', agg_w, x) + agg_b[:, :, None]
        return out

    def _L0_attn_ref(hidden_states, Wqkv, Wo):
        import math
        import jax, jax.numpy as jnp
        import numpy as np
        NUM_HEADS = 32
        HIDDEN = 1024
        HEAD_DIM = HIDDEN // NUM_HEADS
        NEG_INF = -1e+30

        def _alibi_slopes(n: int) -> jnp.ndarray:
            cp2 = 2 ** math.floor(math.log2(n))
            base = 2.0 ** (-2.0 ** (-(math.log2(cp2) - 3)))
            slopes = base ** np.arange(1, cp2 + 1, dtype=np.float64)
            if cp2 != n:
                extra_base = 2.0 ** (-2.0 ** (-(math.log2(2 * cp2) - 3)))
                rem = min(cp2, n - cp2)
                extra = extra_base ** np.arange(1, 1 + 2 * rem, 2, dtype=np.float64)
                slopes = np.concatenate([slopes, extra])
            return jnp.asarray(slopes, dtype=jnp.float32)
        B, S, H = hidden_states.shape
        nH, d = (NUM_HEADS, HEAD_DIM)
        scale = d ** (-0.5)
        qkv = hidden_states @ Wqkv
        q = qkv[..., :nH * d].reshape(B, S, nH, d)
        k = qkv[..., nH * d:nH * d + d]
        v = qkv[..., nH * d + d:]
        scores = jnp.einsum('bqhd,bkd->bhqk', q, k) * scale
        pos_q = jnp.arange(S)[:, None]
        pos_k = jnp.arange(S)[None, :]
        slopes = _alibi_slopes(nH)
        alibi = slopes[:, None, None] * (pos_k - pos_q).astype(jnp.float32)
        causal = pos_k <= pos_q
        scores = jnp.where(causal[None, None], scores + alibi[None], NEG_INF)
        probs = jax.nn.softmax(scores, axis=-1)
        attn = jnp.einsum('bhqk,bkd->bqhd', probs, v).reshape(B, S, H)
        return attn @ Wo

    def _L0_cond2_ref(x, c, weight, c_weight, bias):
        import jax, jax.numpy as jnp
        import numpy as np
        from jax import lax
        N, C_IN, L = (32, 64, 1024)
        C_OUT, K, GROUPS = (64, 9, 4)
        C_DIM, PAD, STRIDE = (128, 4, 1)
        out = lax.conv_general_dilated(x, weight, window_strides=(STRIDE,), padding=[(PAD, PAD)], dimension_numbers=('NCH', 'OIH', 'NCH'), feature_group_count=GROUPS)
        ctx = jnp.einsum('nd,od->no', c, c_weight)
        out = out + ctx[:, :, None] + bias[None, :, None]
        return out

    def _L0_ffn_ref(x, weight, lora_A, lora_B, gw1, gb1, ln_gamma, ln_beta, gw2, gb2):
        import jax, jax.numpy as jnp
        import numpy as np
        B, S, IN, OUT = (4, 512, 1024, 1024)
        E, K, R = (8, 2, 16)
        CAP_FACTOR = 3.0
        ALPHA = 1.0 / R
        LN_EPS = 1e-05
        orig_shape = x.shape
        xf = x.reshape(-1, orig_shape[-1])
        N = xf.shape[0]
        capacity = int(CAP_FACTOR * N / E)
        h = xf @ gw1.T + gb1
        mu = jnp.mean(h, axis=-1, keepdims=True)
        var = jnp.mean((h - mu) ** 2, axis=-1, keepdims=True)
        h = (h - mu) * jax.lax.rsqrt(var + LN_EPS) * ln_gamma + ln_beta
        h = jax.nn.relu(h)
        gates = h @ gw2.T + gb2
        top_v, top_i = jax.lax.top_k(gates, K)
        top_g = jax.nn.softmax(top_v, axis=-1)
        onehot = (top_i[..., None] == jnp.arange(E)).astype(xf.dtype)
        counts = onehot.sum(axis=0)
        allowed = (counts <= capacity).astype(xf.dtype)
        w = jnp.einsum('nke,nk,ke->ne', onehot, top_g, allowed)
        main = xf @ weight.T
        tmp = jnp.einsum('ni,eir->enr', xf, lora_A)
        tmp = tmp * w.T[:, :, None]
        lora = jnp.einsum('enr,ero->no', tmp, lora_B) * ALPHA
        out = main + lora
        return out.reshape(*orig_shape[:-1], weight.shape[0])
    x = x + _L0_attn_ref(_L0_cond_ref(x, cond_128, L0_cond_W0, L0_cond_b0, L0_cond_W1, L0_cond_b1, L0_cond_W2, L0_cond_b2, L0_cond_weight, L0_cond_bias_k), L0_attn_Wqkv, L0_attn_Wo)
    x = x + _L0_ffn_ref(_L0_cond2_ref(x, cond_128, L0_cond2_weight, L0_cond2_c_weight, fside_S_0), L0_ffn_weight, L0_ffn_lora_A, L0_ffn_lora_B, L0_ffn_gw1, L0_ffn_gb1, L0_ffn_ln_gamma, L0_ffn_ln_beta, L0_ffn_gw2, L0_ffn_gb2)
    return x

_drawn_inputs = setup_inputs


def setup_inputs(seed=0):
    import zlib

    import numpy as np

    out = dict(_drawn_inputs(seed))
    spreads = {'L0_cond_b0': (0.0, 0.8),
     'L0_cond_b1': (0.0, 2.0),
     'L0_cond_b2': (0.0, 2.0),
     'L0_ffn_gb1': (0.0, 2.0),
     'L0_ffn_ln_gamma': (1.0, 0.6),
     'L0_ffn_ln_beta': (0.0, 0.575),
     'L0_ffn_gb2': (0.0, 0.314)}
    factors = {'L0_cond_W0': 4.787,
     'L0_cond_W1': 4.411,
     'L0_cond_W2': 4.19,
     'L0_cond_bias_k': 7.667,
     'L0_ffn_gw2': 2.68}
    for name, (base, spread) in spreads.items():
        noise = np.random.default_rng([zlib.crc32(name.encode()), seed]).standard_normal(out[name].shape)
        drawn = base * np.exp(spread * noise) if base else spread * noise
        out[name] = jnp.asarray(drawn.astype(out[name].dtype))
    for name, factor in factors.items():
        out[name] = (out[name] * factor).astype(out[name].dtype)
    return out
```

```python
from contextlib import ExitStack

import numpy as np

import concourse.bass as bass
from concourse import mybir

F32 = mybir.dt.float32
F32R = mybir.dt.float32r
ALU = mybir.AluOpType
ACT = mybir.ActivationFunctionType
AX = mybir.AxisListType

P = 128
BS, CH, L = 32, 64, 1024
PAIRS = BS // 2
KC = L // P
NH, HD = 32, 32
QKV = NH * HD + 2 * HD
EX = 8
R = 16
GH = 4 * EX
LG = EX * R + GH
TAPS, PH = 9, 4
LP = L // PH
N_TOK = BS * CH
CAPACITY = int(3.0 * N_TOK / EX)
HALF = 1024
NEG = -1e30
N_COND = 10
COND_ATT = 4
COND_ROWS = 8
COND_AGG = 5
GATE_VAR = 7
GATE_GAP = 33


def wait_past(eng, semaphore, value):
    if not isinstance(value, int) or value > 0:
        eng.wait_ge(semaphore, value)


def build(nc, xt, xp, emb_t, c_w0, c_b0, c_w1, c_b1, c_w2, c_b2, c_w, c_bk, wq, wkv, wo, tab, ident_d,
          conv_w, cw_t, fside, ffn_w, lg_w, lora_b, gate_c, out):
    agg_d = nc.dram_tensor("agg_d", (BS, CH, CH), F32, kind="Internal").ap()
    aggb_d = nc.dram_tensor("aggb_d", (PAIRS, P), F32, kind="Internal").ap()
    ctxb_d = nc.dram_tensor("ctxb_d", (PAIRS, P), F32, kind="Internal").ap()
    x1_d = nc.dram_tensor("x1_d", (PAIRS, P, L), F32, kind="Internal").ap()

    ctx = ExitStack()
    with ctx:
        def sb(name, shape, dt=F32, stack=ctx):
            return stack.enter_context(nc.sbuf_tensor(name, shape, dt))

        def sem(name):
            return ctx.enter_context(nc.semaphore(name))

        w_hi = sb("w_hi", [P, KC, L], F32R)
        w_lo = sb("w_lo", [P, KC, L], F32R)
        stage = sb("stage", [P, 2, L])
        ident = sb("ident", [P, P])
        wc = sb("wc", [P, 2, 3, P])

        a_mem = ExitStack()
        early = ExitStack()
        cw_sb = sb("cw_sb", [EX, CH * CH], F32, early)
        agg_sb = sb("agg_sb", [BS, CH * CH], F32, early)
        early.close()
        wo_hi = sb("wo_hi", [P, KC, L], F32R, a_mem)
        wo_lo = sb("wo_lo", [P, KC, L], F32R, a_mem)
        tab_sb = sb("tab_sb", [P, NH, CH], F32, a_mem)
        bdagg = sb("bdagg", [P, 2, 2, CH], F32, a_mem)
        aggb = sb("aggb", [P, P], F32, a_mem)
        xt_sb = sb("xt_sb", [P, KC, P], F32, a_mem)
        x_hi = sb("x_hi", [P, KC, P], F32R, a_mem)
        x_lo = sb("x_lo", [P, KC, P], F32R, a_mem)
        xres = sb("xres", [P, L], F32, a_mem)
        wkv_sb = sb("wkv_sb", [P, KC, 2 * HD], F32, a_mem)
        y = sb("y", [P, L], F32, a_mem)
        yk4 = sb("yk4", [P, 4, HD], F32, a_mem)
        yv = sb("yv", [P, HD], F32, a_mem)
        qt = sb("qt", [P, KC, P], F32, a_mem)
        bdk = sb("bdk", [P, 2, 4, CH], F32, a_mem)
        sc = sb("sc", [P, NH, CH], F32, a_mem)
        pt = sb("pt", [P, NH // 2, P], F32, a_mem)
        bdv = sb("bdv", [P, 2, 2 * HD], F32, a_mem)
        early = ExitStack()
        wsum = sb("wsum", [P, QKV], F32, early)
        wsumk4 = sb("wsumk4", [P, 4, HD], F32, early)
        emb_sb = sb("emb_sb", [P, BS], F32, early)
        cwt_sb = sb("cwt_sb", [P, CH], F32, early)
        w0_sb = sb("w0_sb", [P, P], F32, early)
        w1_sb = sb("w1_sb", [P, P], F32, early)
        early.close()
        at_hi = sb("at_hi", [P, KC, P], F32R, a_mem)
        at_lo = sb("at_lo", [P, KC, P], F32R, a_mem)
        ones = sb("ones", [P, P], F32, a_mem)
        cs_q = sb("cs_q", [P, KC + 1], F32, a_mem)
        cs_v = sb("cs_v", [P, HD], F32, a_mem)
        aggb_c = sb("aggb_c", [P, BS], F32, a_mem)
        aggb_p = sb("aggb_p", [P, 2], F32, a_mem)
        mx = sb("mx", [P, NH], F32, a_mem)
        sm = sb("sm", [P, NH], F32, a_mem)
        rs = sb("rs", [P, NH], F32, a_mem)
        b01_sb = sb("b01_sb", [P, 2], F32, a_mem)
        w2_sb = sb("w2_sb", [P, EX], F32, a_mem)
        b2_sb = sb("b2_sb", [BS, EX], F32, a_mem)
        bk_sb = sb("bk_sb", [EX, 2, CH], F32, a_mem)
        fs_sb = sb("fs_sb", [1, CH], F32, a_mem)
        h_sb = sb("h_sb", [P, 2, BS], F32, a_mem)
        att = sb("att", [BS, EX], F32, a_mem)
        att_s = sb("att_s", [BS, 3], F32, a_mem)
        att_t = sb("att_t", [EX, BS], F32, a_mem)
        rows = sb("rows", [BS, 2, CH], F32, a_mem)
        a_mem.close()

        acc = sb("acc", [P, PAIRS, L])
        lgw = sb("lgw", [P, KC, LG])
        x4 = sb("x4", [P, 4, LP + 2])
        ctxb = sb("ctxb", [P, P])
        cv = sb("cv", [P, 2, KC, P])
        cv_hi = sb("cv_hi", [P, 2, KC, P], F32R)
        cv_lo = sb("cv_lo", [P, 2, KC, P], F32R)
        x1r = sb("x1r", [P, L])
        tmp_a = sb("tmp_a", [P, PAIRS, EX * R])
        hg = sb("hg", [P, PAIRS, GH])
        hg2 = sb("hg2", [P, PAIRS, GH])
        lb_sb = sb("lb_sb", [P, L])
        gc = sb("gc", [P, 3 * GH + EX * GH + 2 * EX])
        prod = sb("prod", [P, 4, EX, GH])
        st16 = sb("st16", [P, 6, PAIRS])
        gates = sb("gates", [P, PAIRS, EX])
        hot = sb("hot", [P, 2, PAIRS, EX])
        cand = sb("cand", [P, PAIRS, EX])
        cnt = sb("cnt", [P, 2, EX])
        allow = sb("allow", [P, 2, EX])
        wmix = sb("wmix", [P, PAIRS, EX])
        ones_c = sb("ones_c", [P, P])
        tmpw = sb("tmpw", [P, 2, EX * R])
        tt_sb = sb("tt_sb", [P, 2, P])

        slot = [ctx.enter_context(nc.psum_tensor(f"slot{i}", [P, HALF], F32)) for i in range(3)]
        bank6 = ctx.enter_context(nc.psum_tensor("bank6", [P, 512], F32))
        bank7 = ctx.enter_context(nc.psum_tensor("bank7", [P, 512], F32))

        ld_cond, ld_const, ld_late = sem("ld_cond"), sem("ld_const"), sem("ld_late")
        ld_stage = [sem("ld_stage0"), sem("ld_stage1")]
        ld_xt, ld_agg, ld_aggb, ld_xres = sem("ld_xt"), sem("ld_agg"), sem("ld_aggb"), sem("ld_xres")
        st_rows, st_x1 = sem("st_rows"), sem("st_x1")
        zeroed, cond_pe, cond_act, cond_dve = sem("zeroed"), sem("cond_pe"), sem("cond_act"), sem("cond_dve")
        agg_act, agg_dve = sem("agg_act"), sem("agg_dve")
        w_hi_done, w_lo_done, w_sum_done = sem("w_hi_done"), sem("w_lo_done"), sem("w_sum_done")
        wsum_kv, cs_psum, cs_ready = sem("wsum_kv"), sem("cs_psum"), sem("cs_ready")
        x_hi_ready, x_lo_ready, y_psum, y_ready = sem("x_hi_ready"), sem("x_lo_ready"), sem("y_psum"), sem("y_ready")
        qt_psum, qt_ready, vv_psum = sem("qt_psum"), sem("qt_ready"), sem("vv_psum")
        aggb_picked, bdv_ready = sem("aggb_picked"), sem("bdv_ready")
        score_psum, score_ready, max_ready = sem("score_psum"), sem("score_ready"), sem("max_ready")
        shifted, exp_ready, sum_ready = sem("shifted"), sem("exp_ready"), sem("sum_ready")
        rsum_ready, prob_ready, pt_psum, pt_ready = sem("rsum_ready"), sem("prob_ready"), sem("pt_psum"), sem("pt_ready")
        at_psum, at_hi_ready, at_lo_ready = sem("at_psum"), sem("at_hi_ready"), sem("at_lo_ready")
        wo_psum, x1_ready = sem("wo_psum"), sem("x1_ready")
        ld_b, ld_x4, ld_ctx, ld_x1r, st_out = sem("ld_b"), sem("ld_x4"), sem("ld_ctx"), sem("ld_x1r"), sem("st_out")
        pads_zero, conv_psum, cv_ready = sem("pads_zero"), sem("conv_psum"), sem("cv_ready")
        cv_hi_ready, cv_lo_ready, lg_psum, lg_ready = sem("cv_hi_ready"), sem("cv_lo_ready"), sem("lg_psum"), sem("lg_ready")
        main_psum, acc_ready = sem("main_psum"), sem("acc_ready")
        gate_dve, gate_act, cnt_hot, cnt_psum, wmix_ready = sem("gate_dve"), sem("gate_act"), sem("cnt_hot"), sem("cnt_psum"), sem("wmix_ready")
        tmpw_ready, tt_psum, tt_ready, lb_psum, out_ready = sem("tmpw_ready"), sem("tt_psum"), sem("tt_ready"), sem("lb_psum"), sem("out_ready")

        LAST = PAIRS - 1
        flat = "p a b -> p (a b)"
        block = ctx.enter_context(nc.Block())

        @block.sync
        def _(sp):
            conds = ((emb_sb[:], emb_t), (w0_sb[:], c_w0), (b01_sb[:, 0:1], c_b0), (w1_sb[:], c_w1),
                     (b01_sb[:, 1:2], c_b1), (w2_sb[:], c_w2), (b2_sb[:], c_b2), (bk_sb[:], c_bk),
                     (cwt_sb[:], cw_t), (fs_sb[:], fside))
            assert len(conds) == N_COND
            for t, s in conds:
                sp.dma_start(t, s).then_inc(ld_cond, 16)
            sp.dma_start(ident[:], ident_d).then_inc(ld_const, 16)
            sp.dma_start(cw_sb[:], c_w).then_inc(ld_const, 16)
            sp.dma_start(xt_sb[:], xt[0]).then_inc(ld_xt, 16)

            def stage_in(n, src):
                if n >= 2:
                    sp.wait_ge(w_hi_done, n - 1)
                    sp.wait_ge(w_lo_done, n - 1)
                    sp.wait_ge(w_sum_done, min(n - 1, KC))
                sp.dma_start(stage[:, n % 2, :], src).then_inc(ld_stage[n % 2], 16)

            for c in range(KC):
                stage_in(c, wq[c])
            sp.dma_start(wkv_sb[:], wkv).then_inc(ld_late, 16)
            sp.dma_start(tab_sb[:], tab).then_inc(ld_late, 16)
            sp.dma_start(wc[:], conv_w).then_inc(ld_late, 16)
            sp.wait_ge(agg_act, 2)
            sp.wait_ge(agg_dve, 2)
            sp.dma_start(agg_d.rearrange("b i o -> b (i o)"), agg_sb[:]).then_inc(st_rows, 16)
            sp.wait_ge(cond_dve, COND_ROWS)
            sp.dma_start(aggb_d.rearrange("n (b o) -> (n b) o", b=2), rows[:, 0, :]).then_inc(st_rows, 16)
            sp.dma_start(ctxb_d.rearrange("n (b o) -> (n b) o", b=2), rows[:, 1, :]).then_inc(st_rows, 16)
            sp.wait_ge(st_rows, 48)
            sp.wait_ge(zeroed, 4)

            def load_agg(n):
                for b in range(2):
                    for r in range(2):
                        sp.dma_start(bdagg[CH * b:CH * b + CH, b, r, :], agg_d[2 * n + b]).then_inc(ld_agg, 16)
                sp.dma_start(aggb[:], aggb_d[n].partition_broadcast(P)).then_inc(ld_aggb, 16)

            load_agg(0)
            for c in range(KC):
                stage_in(KC + c, wo[c])

            def next_loads(i):
                sp.wait_ge(y_psum, i + 1)
                sp.dma_start(xt_sb[:], xt[i + 1]).then_inc(ld_xt, 16)
                sp.wait_ge(vv_psum, i + 1)
                sp.wait_ge(qt_ready, i + 1)
                load_agg(i + 1)

            def residual(n):
                wait_past(sp, st_x1, 16 * n)
                sp.dma_start(xres[:], xp[n]).then_inc(ld_xres, 16)

            def store_x1(n):
                sp.wait_ge(x1_ready, n + 1)
                sp.dma_start(x1_d[n], xres[:]).then_inc(st_x1, 16)

            def a_loads(i):
                next_loads(i)
                residual(i - 1)
                store_x1(i - 1)

            next_loads(0)
            a_loads(1)
            with sp.Fori(2, LAST) as i:
                a_loads(i)

            residual(LAST - 1)
            sp.wait_ge(y_psum, PAIRS)
            for c in range(KC):
                stage_in(2 * KC + c, ffn_w[c])
            store_x1(LAST - 1)
            residual(LAST)
            store_x1(LAST)
            sp.wait_ge(st_x1, 16 * PAIRS)

            for t, s in ((lgw[:], lg_w), (lb_sb[:], lora_b), (gc[:], gate_c)):
                sp.dma_start(t, s).then_inc(ld_b, 16)
            sp.wait_ge(pads_zero, 1)

            def load_x4(n):
                for ph in range(PH):
                    sp.dma_start(x4[32 * ph:32 * ph + 32, :, 1:LP + 1],
                                 x1_d[n][:, LP * ph:LP * ph + LP].rearrange("(g c) l -> c g l", g=4)
                                 ).then_inc(ld_x4, 16)

            def load_ctx(n):
                sp.dma_start(ctxb[:], ctxb_d[n].partition_broadcast(P)).then_inc(ld_ctx, 16)

            load_x4(0)
            load_ctx(0)

            def b_next(n):
                sp.wait_ge(conv_psum, n + 1)
                load_x4(n + 1)
                sp.wait_ge(cv_ready, n + 1)
                load_ctx(n + 1)

            def b_residual(n):
                wait_past(sp, acc_ready, n)
                sp.dma_start(x1r[:], x1_d[n]).then_inc(ld_x1r, 16)

            b_next(0)
            b_residual(0)
            with sp.Fori(1, LAST) as i:
                b_next(i)
                b_residual(i)
            b_residual(LAST)

            with sp.Fori(0, PAIRS) as i:
                sp.wait_ge(out_ready, i + 1)
                sp.dma_start(out[i], acc[:, bass.ds(i, 1), :].rearrange("p a n -> p (a n)")).then_inc(st_out, 16)
            sp.wait_ge(st_out, 16 * PAIRS)

        @block.tensor
        def _(pe):
            def split_product(dst, a_hi, a_lo, b_hi, b_lo, before=lambda c: None):
                for c in range(KC):
                    before(c)
                    for t, (a, b) in enumerate(((a_hi, b_hi), (a_hi, b_lo), (a_lo, b_hi))):
                        for k in range(2):
                            m = pe.matmul(dst[:, 512 * k:512 * k + 512], a(c), b[:, c, 512 * k:512 * k + 512],
                                          start=(c == 0 and t == 0), stop=(c == KC - 1 and t == 2))
                return m

            pe.wait_ge(ld_cond, 16 * N_COND)
            pe.matmul(bank7[:, 0:BS], w0_sb[:], emb_sb[:], start=True, stop=True).then_inc(cond_pe, 1)
            pe.wait_ge(cond_act, 1)
            pe.matmul(bank7[:, BS:2 * BS], w1_sb[:], h_sb[:, 0, :], start=True, stop=True).then_inc(cond_pe, 1)
            pe.wait_ge(cond_act, 2)
            pe.matmul(bank7[0:BS, 64:64 + EX], h_sb[:, 1, :], w2_sb[:], start=True, stop=True).then_inc(cond_pe, 1)
            pe.wait_ge(cond_dve, COND_ATT)
            pe.wait_ge(ld_const, 32)
            pe.transpose(bank7[0:EX, 128:128 + BS], att[:], ident[0:BS, 0:BS]).then_inc(cond_pe, 1)
            pe.wait_ge(cond_dve, COND_ATT + 1)
            pe.wait_ge(zeroed, 4)
            pe.matmul(bank7[0:BS, 192:192 + CH], att_t[:], bk_sb[:, 0, :], start=True, stop=True)
            pe.matmul(bank7[:, 256:256 + BS], bk_sb[:, :, :].rearrange(flat), att_t[:], start=True, stop=True)
            pe.matmul(bank7[0:BS, 320:320 + CH], ones[0:1, 0:BS], fs_sb[:], start=True, stop=False)
            pe.matmul(bank7[0:BS, 320:320 + CH], emb_sb[:], cwt_sb[:], start=False, stop=True).then_inc(cond_pe, 1)
            for g in range(4):
                if g == 3:
                    pe.wait_ge(agg_act, 1)
                for k in range(2):
                    at = HALF * g + 512 * k
                    m = pe.matmul(slot[g % 3][0:BS, 512 * k:512 * k + 512], att_t[:], cw_sb[:, at:at + 512],
                                  start=True, stop=True)
                m.then_inc(cond_pe, 1)

            def products(n, before=lambda c: None):
                pe.wait_ge(x_hi_ready, n + 1)
                pe.wait_ge(x_lo_ready, n + 1)
                split_product(slot[2], lambda c: x_hi[:, c, :], lambda c: x_lo[:, c, :], w_hi, w_lo, before)
                for c in range(KC):
                    m = pe.matmul(bank6[:, 0:2 * HD], xt_sb[:, c, :], wkv_sb[:, c, :],
                                  start=(c == 0), stop=(c == KC - 1))
                m.then_inc(y_psum, 1)

            def mix_q(n):
                pe.wait_ge(y_ready, n + 1)
                pe.wait_ge(ld_agg, 64 * (n + 1))
                for c in range(KC):
                    pe.matmul(slot[2][:, P * c:P * c + P].rearrange("p (b o) -> p b o", b=2),
                              y[:, P * c:P * c + P], bdagg[:, :, 0, :], start=True, stop=True)
                pe.matmul(bank6[:, P:2 * P].rearrange("p (b o) -> p b o", b=2), yk4[:, :, :].rearrange(flat),
                          bdagg[:, :, 0, :], start=True, stop=True).then_inc(qt_psum, 1)

            def mix_v(n):
                for b in range(2):
                    m = pe.matmul(bank7[:, HD * b:HD * b + HD], bdagg[:, b, :, :].rearrange(flat), yv[:],
                                  start=True, stop=True)
                m.then_inc(vv_psum, 1)

            def scores(i):
                pe.wait_ge(qt_ready, i + 1)
                for hh in range(2):
                    for c in range(4):
                        for b in range(2):
                            m = pe.matmul(slot[hh][CH * b:CH * b + CH, 256 * c:256 * c + 256],
                                          qt[:, 4 * hh + c, CH * b:CH * b + CH],
                                          bdk[:, b, :, :].rearrange(flat), start=True, stop=True)
                    m.then_inc(score_psum, 1)

            def turn_probs(i):
                for hh in range(2):
                    pe.wait_ge(prob_ready, 2 * i + hh + 1)
                    for k in range(8):
                        h = 16 * hh + 2 * k
                        m = pe.transpose(slot[hh][:, P * k:P * k + P], sc[:, h:h + 2, :].rearrange(flat), ident[:])
                    m.then_inc(pt_psum, 1)

            def attend(i):
                pe.wait_ge(pt_ready, 2 * i + 2)
                pe.wait_ge(bdv_ready, i + 1)
                for b in range(2):
                    for eo in range(2):
                        m = pe.matmul(slot[2][CH * eo:CH * eo + CH, 512 * b:512 * b + 512]
                                      .rearrange("p (c t) -> p c t", c=KC), bdv[:, b, :],
                                      pt[:, eo::2, CH * b:CH * b + CH], start=True, stop=True)
                m.then_inc(at_psum, 1)

            def project(n):
                pe.wait_ge(at_hi_ready, n + 1)
                pe.wait_ge(at_lo_ready, n + 1)
                split_product(slot[1], lambda c: at_hi[:, c, :], lambda c: at_lo[:, c, :], wo_hi, wo_lo
                              ).then_inc(wo_psum, 1)

            def chunk_split(c):
                pe.wait_ge(w_hi_done, c + 1)
                pe.wait_ge(w_lo_done, c + 1)

            pe.wait_ge(agg_act, 2)
            pe.wait_ge(ld_late, 48)
            products(0, chunk_split)
            pe.wait_ge(wsum_kv, 2)
            pe.wait_ge(w_sum_done, KC)
            pe.wait_ge(cond_dve, COND_ROWS)
            for c in range(KC):
                pe.matmul(bank7[:, 128 + c:129 + c], wsum[:, P * c:P * c + P], ones[:, 0:1], start=True, stop=True)
            pe.matmul(bank7[:, 136:137], wsumk4[:, :, :].rearrange(flat), ones[:, 0:1], start=True, stop=True)
            pe.matmul(bank7[:, 160:160 + HD], ones[:], wsum[:, L + HD:QKV], start=True, stop=True
                      ).then_inc(cs_psum, 1)
            mix_q(0)
            pe.wait_ge(cs_ready, 2)
            mix_v(0)

            def pair(i, first=False):
                wait_past(pe, x1_ready, i - 1)
                scores(i)
                wait_past(pe, at_lo_ready, i)
                products(i + 1)
                turn_probs(i)
                mix_q(i + 1)
                if not first:
                    pe.wait_ge(pt_ready, 2 * i + 2)
                    project(i - 1)
                pe.wait_ge(qt_ready, i + 2)
                attend(i)
                mix_v(i + 1)

            pe.wait_ge(agg_dve, 2)
            pair(0, True)
            chunk_split(2 * KC - 1)
            pair(1)
            with pe.Fori(2, LAST) as i:
                pair(i)
            pe.wait_ge(x1_ready, LAST - 1)
            scores(LAST)
            pe.wait_ge(score_ready, 2 * PAIRS)
            project(LAST - 1)
            pe.wait_ge(x1_ready, LAST)
            turn_probs(LAST)
            pe.wait_ge(at_lo_ready, LAST)
            attend(LAST)
            project(LAST)

            def conv(n):
                pe.wait_ge(ld_x4, 64 * (n + 1))
                for g in range(4):
                    for j in range(2):
                        for s in range(3):
                            m = pe.matmul(slot[0][:, 512 * j:512 * j + 512].rearrange("p (a t) -> p a t", a=PH)
                                          [:, :, 32 * g:32 * g + 32],
                                          x4[:, g, P * j + s:P * j + s + P], wc[:, g % 2, s, :],
                                          start=(s == 0), stop=(s == 2))
                m.then_inc(conv_psum, 1)

            def dense(n, u):
                pe.wait_ge(cv_ready, n + 1)
                wait_past(pe, lg_ready, n)
                for c in range(KC):
                    m = pe.matmul(bank6[:, 0:LG], cv[:, u, c, :], lgw[:, c, :], start=(c == 0), stop=(c == KC - 1))
                m.then_inc(lg_psum, 1)
                pe.wait_ge(cv_hi_ready, n + 1)
                pe.wait_ge(cv_lo_ready, n + 1)
                wait_past(pe, acc_ready, n)
                split_product(slot[1], lambda c: cv_hi[:, u, c, :], lambda c: cv_lo[:, u, c, :], w_hi, w_lo
                              ).then_inc(main_psum, 1)

            pe.wait_ge(ld_b, 48)
            pe.wait_ge(x1_ready, PAIRS)
            conv(0)
            chunk_split(3 * KC - 1)

            def two_pairs(i):
                for u in range(2):
                    pe.wait_ge(cv_ready, 2 * i + u + 1)
                    conv(2 * i + u + 1)
                    dense(2 * i + u, u)

            two_pairs(0)
            with pe.Fori(1, PAIRS // 2 - 1) as i:
                two_pairs(i)
            pe.wait_ge(cv_ready, LAST)
            conv(LAST)
            dense(LAST - 1, 0)
            dense(LAST, 1)

            pe.wait_ge(cnt_hot, 1)
            pe.wait_ge(lg_ready, PAIRS)
            pe.matmul(bank6[:, 256:256 + 2 * EX], ones_c[:], cnt[:, :, :].rearrange(flat), start=True, stop=True
                      ).then_inc(cnt_psum, 1)
            turned = [bank6, bank7]

            def lora(i, first=False):
                for u in range(2):
                    pe.wait_ge(tmpw_ready, 2 * i + u + 1)
                    pe.transpose(turned[u][:, 0:P], tmpw[:, u, :], ident[:]).then_inc(tt_psum, 1)
                for u in range(2):
                    n = 2 * i + u
                    pe.wait_ge(tt_ready, n + 1)
                    if not first:
                        pe.wait_ge(out_ready, n - 1)
                    for k in range(2):
                        m = pe.matmul(slot[u][:, 512 * k:512 * k + 512], tt_sb[:, u, :],
                                      lb_sb[:, 512 * k:512 * k + 512], start=True, stop=True)
                    m.then_inc(lb_psum, 1)

            pe.wait_ge(acc_ready, PAIRS)
            lora(0, True)
            with pe.Fori(1, PAIRS // 2) as i:
                lora(i)

        @block.scalar
        def _(act):
            act.wait_ge(ld_cond, 16 * N_COND)
            for t in range(2):
                act.wait_ge(cond_pe, t + 1)
                act.activation(h_sb[:, t, :], bank7[:, BS * t:BS * t + BS], ACT.Gelu, bias=b01_sb[:, t:t + 1]
                               ).then_inc(cond_act, 1)
            act.wait_ge(cond_dve, 2)
            act.activation(att[:], att[:], ACT.Exp, bias=att_s[:, 0:1], accum_out=att_s[:, 1:2]).then_inc(cond_act, 1)

            def split_hi(n, dst, c):
                act.wait_ge(ld_stage[n % 2], 16 * (n // 2 + 1))
                act.activation(dst[:, c, :], stage[:, n % 2, :], ACT.Copy).then_inc(w_hi_done, 1)

            def x_high(n):
                act.wait_ge(ld_xt, 16 * (n + 1))
                act.activation(x_hi[:], xt_sb[:], ACT.Copy).then_inc(x_hi_ready, 1)

            def y_copy(n):
                act.wait_ge(y_psum, n + 1)
                act.activation(y[:], slot[2][:], ACT.Copy)
                act.activation(yk4[:], bank6[:, 0:HD].unsqueeze(1).to_broadcast([P, 4, HD]), ACT.Copy)
                act.activation(yv[:], bank6[:, HD:2 * HD], ACT.Copy).then_inc(y_ready, 1)

            def exps(i):
                for hh in range(2):
                    act.wait_ge(shifted, 2 * i + hh + 1)
                    half = sc[:, 16 * hh:16 * hh + 16, :]
                    act.activation(half, half, ACT.Exp).then_inc(exp_ready, 1)

            def pt_copy(i):
                for hh in range(2):
                    act.wait_ge(pt_psum, 2 * i + hh + 1)
                    act.activation(pt[:, 8 * hh:8 * hh + 8, :], slot[hh][:].rearrange("p (h t) -> p h t", h=8),
                                   ACT.Copy).then_inc(pt_ready, 1)

            def at_high(i):
                act.wait_ge(at_psum, i + 1)
                act.activation(at_hi[:, :, :].rearrange("p c (b t) -> p b c t", b=2),
                               slot[2][:].rearrange("p (b c t) -> p b c t", b=2, c=KC), ACT.Copy
                               ).then_inc(at_hi_ready, 1)

            x_high(0)
            for c in range(2):
                split_hi(c, w_hi, c)
            for g in (0, 2):
                act.wait_ge(cond_pe, COND_AGG + g + 1)
                act.activation(agg_sb[:, HALF * g:HALF * g + HALF], slot[g % 3][0:BS, :], ACT.Copy
                               ).then_inc(agg_act, 1)
            for c in range(2, KC):
                split_hi(c, w_hi, c)
            y_copy(0)
            act.wait_ge(st_rows, 48)
            act.wait_ge(cond_pe, COND_AGG + 4)
            for c in range(KC):
                split_hi(KC + c, wo_hi, c)
            x_high(1)

            def pair(i, more=True):
                exps(i)
                y_copy(i + 1)
                pt_copy(i)
                at_high(i)
                if more:
                    x_high(i + 2)

            with act.Fori(0, LAST - 1) as i:
                pair(i)
            pair(LAST - 1, False)
            exps(LAST)
            for c in range(KC):
                split_hi(2 * KC + c, w_hi, c)
            pt_copy(LAST)
            at_high(LAST)

            def conv_high(n, u):
                act.wait_ge(cv_ready, n + 1)
                act.activation(cv_hi[:, u, :, :], cv[:, u, :, :], ACT.Copy).then_inc(cv_hi_ready, 1)

            def lg_copy(n):
                act.wait_ge(lg_psum, n + 1)
                act.activation(tmp_a[:, bass.ds(n, 1), :], bank6[:, 0:EX * R].unsqueeze(1), ACT.Copy)
                act.activation(hg[:, bass.ds(n, 1), :], bank6[:, EX * R:LG].unsqueeze(1), ACT.Copy
                               ).then_inc(lg_ready, 1)

            conv_high(0, 0)

            def two_pairs(i):
                for u in range(2):
                    lg_copy(2 * i + u)
                    wait_past(act, main_psum, 2 * i + u)
                    conv_high(2 * i + u + 1, 1 - u)

            two_pairs(0)
            with act.Fori(1, PAIRS // 2 - 1) as i:
                two_pairs(i)
            lg_copy(LAST - 1)
            act.wait_ge(main_psum, LAST - 1)
            conv_high(LAST, 1)
            lg_copy(LAST)

            act.wait_ge(gate_dve, GATE_VAR)
            act.activation(st16[:, 1, :], st16[:, 1, :], ACT.Sqrt).then_inc(gate_act, 1)
            act.wait_ge(gate_dve, GATE_GAP)
            act.activation(st16[:, 4, :], st16[:, 4, :], ACT.Exp).then_inc(gate_act, 1)
            turned = [bank6, bank7]

            def turned_copy(i):
                for u in range(2):
                    act.wait_ge(tt_psum, 2 * i + u + 1)
                    wait_past(act, lb_psum, 2 * i)
                    act.activation(tt_sb[:, u, :], turned[u][:, 0:P], ACT.Copy).then_inc(tt_ready, 1)

            turned_copy(0)
            with act.Fori(1, PAIRS // 2) as i:
                turned_copy(i)

        @block.gpsimd
        def _(pool):
            for t, v in ((bdagg, 0.0), (bdk, 0.0), (bdv, 0.0), (ones, 1.0)):
                pool.memset(t[:], v).then_inc(zeroed, 1)

            def x_low(n):
                pool.wait_ge(x_hi_ready, n + 1)
                pool.tensor_tensor(x_lo[:], xt_sb[:], x_hi[:].bitcast(F32), ALU.subtract).then_inc(x_lo_ready, 1)

            x_low(0)
            for c in range(KC):
                pool.wait_ge(ld_stage[c % 2], 16 * (c // 2 + 1))
                if c == 0:
                    pool.tensor_copy(wsum[:, 0:L], stage[:, 0, :]).then_inc(w_sum_done, 1)
                else:
                    pool.wait_ge(w_sum_done, c)
                    pool.tensor_tensor(wsum[:, 0:L], wsum[:, 0:L], stage[:, c % 2, :], ALU.add).then_inc(w_sum_done, 1)
            pool.wait_ge(y_psum, 1)
            x_low(1)

            def shift_and_norm(i):
                for t, (ready, op, done) in enumerate(((max_ready, ALU.subtract, shifted), (rsum_ready, ALU.mult, prob_ready))):
                    v = (mx, rs)[t]
                    for hh in range(2):
                        pool.wait_ge(ready, 2 * i + hh + 1)
                        half = sc[:, 16 * hh:16 * hh + 16, :]
                        pool.tensor_tensor(half, half, v[:, 16 * hh:16 * hh + 16].unsqueeze(2)
                                           .to_broadcast([P, 16, CH]), op).then_inc(done, 1)

            with pool.Fori(0, LAST - 1) as i:
                shift_and_norm(i)
                x_low(i + 2)
            shift_and_norm(LAST - 1)
            shift_and_norm(LAST)

            def conv_low(n, u):
                pool.wait_ge(cv_hi_ready, n + 1)
                pool.tensor_tensor(cv_lo[:, u, :, :], cv[:, u, :, :], cv_hi[:, u, :, :].bitcast(F32), ALU.subtract
                                   ).then_inc(cv_lo_ready, 1)

            with pool.Fori(0, PAIRS // 2) as i:
                for u in range(2):
                    conv_low(2 * i + u, u)

            pool.wait_ge(wmix_ready, 1)
            pool.wait_ge(lg_ready, PAIRS)

            def weigh(n, u):
                pool.tensor_tensor(tmpw[:, u, :].rearrange("p (a e r) -> p a e r", a=1, r=R),
                                   tmp_a[:, bass.ds(n, 1), :].rearrange("p a (e r) -> p a e r", r=R),
                                   wmix[:, bass.ds(n, 1), :].unsqueeze(3).to_broadcast([P, 1, EX, R]), ALU.mult
                                   ).then_inc(tmpw_ready, 1)

            weigh(0, 0)
            weigh(1, 1)
            with pool.Fori(1, PAIRS // 2) as i:
                for u in range(2):
                    pool.wait_ge(tt_psum, 2 * i + u - 1)
                    weigh(2 * i + u, u)

        @block.vector
        def _(dve):
            def cond(ins, value):
                ins.then_inc(cond_dve, 1)
                dve.wait_ge(cond_dve, value)

            dve.wait_ge(cond_pe, 3)
            dve.wait_ge(ld_cond, 16 * N_COND)
            cond(dve.tensor_tensor(att[:], bank7[0:BS, 64:64 + EX], b2_sb[:], ALU.add), 1)
            cond(dve.tensor_reduce(att_s[:, 0:1], att[:], AX.X, ALU.max, negate=True), 2)
            dve.wait_ge(cond_act, 3)
            cond(dve.reciprocal(att_s[:, 2:3], att_s[:, 1:2]), 3)
            cond(dve.tensor_scalar(att[:], att[:], att_s[:, 2:3], None, ALU.mult), COND_ATT)
            dve.wait_ge(cond_pe, 4)
            cond(dve.tensor_copy(att_t[:], bank7[0:EX, 128:128 + BS]), COND_ATT + 1)
            dve.wait_ge(cond_pe, COND_AGG)
            dve.tensor_copy(rows[:, 0, :], bank7[0:BS, 192:192 + CH]).then_inc(cond_dve, 1)
            dve.tensor_copy(rows[:, 1, :], bank7[0:BS, 320:320 + CH]).then_inc(cond_dve, 1)
            dve.tensor_copy(aggb_c[:], bank7[:, 256:256 + BS]).then_inc(cond_dve, 1)

            def split_lo(n, dst_hi, dst_lo, c):
                dve.wait_ge(w_hi_done, n + 1)
                dve.tensor_tensor(dst_lo[:, c, :], stage[:, n % 2, :], dst_hi[:, c, :].bitcast(F32), ALU.subtract
                                  ).then_inc(w_lo_done, 1)

            split_lo(0, w_hi, w_lo, 0)
            split_lo(1, w_hi, w_lo, 1)
            for g in (1, 3):
                dve.wait_ge(cond_pe, COND_AGG + g + 1)
                dve.tensor_copy(agg_sb[:, HALF * g:HALF * g + HALF], slot[g % 3][0:BS, :]).then_inc(agg_dve, 1)
            for c in range(2, KC):
                split_lo(c, w_hi, w_lo, c)
            dve.wait_ge(ld_late, 48)
            dve.tensor_reduce(wsum[:, L:QKV], wkv_sb[:].rearrange("p c n -> p n c"), AX.X, ALU.add).then_inc(wsum_kv, 1)
            dve.wait_ge(wsum_kv, 1)
            dve.tensor_copy(wsumk4[:], wsum[:, L:L + HD].unsqueeze(1).to_broadcast([P, 4, HD])).then_inc(wsum_kv, 1)
            dve.wait_ge(cs_psum, 1)
            dve.tensor_copy(cs_q[:], bank7[:, 128:128 + KC + 1]).then_inc(cs_ready, 1)
            dve.tensor_copy(cs_v[:], bank7[:, 160:160 + HD]).then_inc(cs_ready, 1)
            dve.wait_ge(cs_ready, 2)

            def mixed_q(n):
                dve.wait_ge(qt_psum, n + 1)
                dve.wait_ge(ld_aggb, 16 * (n + 1))
                for c in range(KC):
                    dve.scalar_tensor_tensor(out=qt[:, c, :], in0=aggb[:], scalar=cs_q[:, c:c + 1],
                                             in1=slot[2][:, P * c:P * c + P], op0=ALU.mult, op1=ALU.add)
                for j in range(4):
                    q = slice(32 * j, 32 * j + 32)
                    last = dve.scalar_tensor_tensor(
                        out=bdk[q, :, j, :], in0=aggb[q, :].rearrange("p (b k) -> p b k", b=2),
                        scalar=cs_q[q, KC:KC + 1], in1=bank6[q, P:2 * P].rearrange("p (b k) -> p b k", b=2),
                        op0=ALU.mult, op1=ALU.add)
                last.then_inc(qt_ready, 1)

            def mixed_v(n):
                dve.wait_ge(vv_psum, n + 1)
                dve.tensor_copy(aggb_p[:], aggb_c[:, bass.ds(2 * n, 2)]).then_inc(aggb_picked, 1)
                dve.wait_ge(aggb_picked, n + 1)
                for b in range(2):
                    for r in range(2):
                        q = slice(CH * r, CH * r + CH)
                        last = dve.scalar_tensor_tensor(
                            out=bdv[q, b, HD * r:HD * r + HD], in0=cs_v[q, :], scalar=aggb_p[q, b:b + 1],
                            in1=bank7[q, HD * b:HD * b + HD], op0=ALU.mult, op1=ALU.add)
                last.then_inc(bdv_ready, 1)

            dve.wait_ge(zeroed, 4)
            dve.wait_ge(cond_dve, COND_ROWS)
            mixed_q(0)
            mixed_v(0)
            for c in range(KC):
                split_lo(KC + c, wo_hi, wo_lo, c)

            def softmax_parts(i):
                for hh in range(2):
                    half = sc[:, 16 * hh:16 * hh + 16, :]
                    dve.wait_ge(score_psum, 2 * i + hh + 1)
                    dve.scalar_tensor_tensor(out=half, in0=slot[hh][:].rearrange("p (h k) -> p h k", h=16),
                                             scalar=HD ** -0.5, in1=tab_sb[:, 16 * hh:16 * hh + 16, :],
                                             op0=ALU.mult, op1=ALU.add).then_inc(score_ready, 1)
                    dve.wait_ge(score_ready, 2 * i + hh + 1)
                    dve.tensor_reduce(mx[:, 16 * hh:16 * hh + 16], half, AX.X, ALU.max).then_inc(max_ready, 1)
                for hh in range(2):
                    half = sc[:, 16 * hh:16 * hh + 16, :]
                    dve.wait_ge(exp_ready, 2 * i + hh + 1)
                    dve.tensor_reduce(sm[:, 16 * hh:16 * hh + 16], half, AX.X, ALU.add).then_inc(sum_ready, 1)
                    dve.wait_ge(sum_ready, 2 * i + hh + 1)
                    dve.reciprocal(rs[:, 16 * hh:16 * hh + 16], sm[:, 16 * hh:16 * hh + 16]).then_inc(rsum_ready, 1)

            def residual(n):
                dve.wait_ge(wo_psum, n + 1)
                dve.wait_ge(ld_xres, 16 * (n + 1))
                dve.tensor_tensor(xres[:], slot[1][:], xres[:], ALU.add).then_inc(x1_ready, 1)

            def at_low(i):
                dve.wait_ge(at_hi_ready, i + 1)
                split = "p c (b t) -> p b c t"
                dve.tensor_tensor(at_lo[:, :, :].rearrange(split, b=2),
                                  slot[2][:].rearrange("p (b c t) -> p b c t", b=2, c=KC),
                                  at_hi[:, :, :].bitcast(F32).rearrange(split, b=2), ALU.subtract
                                  ).then_inc(at_lo_ready, 1)

            softmax_parts(0)
            mixed_q(1)
            at_low(0)
            mixed_v(1)
            with dve.Fori(1, LAST) as i:
                softmax_parts(i)
                mixed_q(i + 1)
                residual(i - 1)
                at_low(i)
                mixed_v(i + 1)
            softmax_parts(LAST)
            for c in range(KC):
                split_lo(2 * KC + c, w_hi, w_lo, c)
            residual(LAST - 1)
            at_low(LAST)
            residual(LAST)

            dve.wait_ge(st_x1, 16 * PAIRS)
            dve.memset(ones_c[:], 1.0)
            dve.memset(x4[:, :, 0:1], 0.0)
            dve.memset(x4[:, :, LP + 1:LP + 2], 0.0).then_inc(pads_zero, 1)

            def conv_sum(n, u):
                dve.wait_ge(conv_psum, n + 1)
                dve.wait_ge(ld_ctx, 16 * (n + 1))
                dve.tensor_tensor(cv[:, u, :, :], slot[0][:].rearrange("p (c t) -> p c t", c=KC),
                                  ctxb[:].unsqueeze(1).to_broadcast([P, KC, P]), ALU.add).then_inc(cv_ready, 1)

            def dense_sum(n):
                dve.wait_ge(main_psum, n + 1)
                dve.wait_ge(ld_x1r, 16 * (n + 1))
                dve.tensor_tensor(acc[:, bass.ds(n, 1), :], slot[1][:].unsqueeze(1), x1r[:].unsqueeze(1), ALU.add
                                  ).then_inc(acc_ready, 1)

            conv_sum(0, 0)
            conv_sum(1, 1)
            dense_sum(0)
            with dve.Fori(0, PAIRS // 2 - 1) as i:
                for u in range(2):
                    n = 2 * i + u + 1
                    dve.wait_ge(cv_lo_ready, n)
                    conv_sum(n + 1, u)
                    dense_sum(n)
            dense_sum(LAST)

            steps = [0]

            def step(ins):
                steps[0] += 1
                ins.then_inc(gate_dve, 1)
                dve.wait_ge(gate_dve, steps[0])

            def wide(t, n=GH):
                return t.unsqueeze(2).to_broadcast([P, PAIRS, n])

            def row(t, n):
                return t.unsqueeze(1).to_broadcast([P, PAIRS, n])

            gb1, gamma, beta = (gc[:, GH * t:GH * t + GH] for t in range(3))
            gw2 = gc[:, 3 * GH:3 * GH + EX * GH].rearrange("p (e h) -> p e h", e=EX)
            gb2 = gc[:, 3 * GH + EX * GH:3 * GH + EX * GH + EX]
            rank = gc[:, 3 * GH + EX * GH + EX:3 * GH + EX * GH + 2 * EX]
            mean, var, top1, top2, gap, inv = (st16[:, t, :] for t in range(6))
            dve.wait_ge(lg_ready, PAIRS)
            dve.wait_ge(ld_b, 48)
            step(dve.tensor_tensor(hg[:], hg[:], row(gb1, GH), ALU.add))
            step(dve.tensor_reduce(mean, hg[:], AX.X, ALU.add))
            step(dve.tensor_scalar(mean, mean, 1.0 / GH, None, ALU.mult))
            step(dve.tensor_tensor(hg[:], hg[:], wide(mean), ALU.subtract))
            step(dve.tensor_tensor(hg2[:], hg[:], hg[:], ALU.mult))
            step(dve.tensor_reduce(var, hg2[:], AX.X, ALU.add))
            step(dve.tensor_scalar(var, var, 1.0 / GH, 1e-5, ALU.mult, ALU.add))
            assert steps[0] == GATE_VAR
            dve.wait_ge(gate_act, 1)
            step(dve.reciprocal(mean, var))
            step(dve.tensor_tensor(hg[:], hg[:], wide(mean), ALU.mult))
            step(dve.tensor_tensor(hg[:], hg[:], row(gamma, GH), ALU.mult))
            step(dve.tensor_tensor(hg[:], hg[:], row(beta, GH), ALU.add))
            step(dve.tensor_scalar(hg[:], hg[:], 0.0, None, ALU.max))
            for q in range(4):
                four = hg[:, 4 * q:4 * q + 4, :]
                step(dve.tensor_tensor(prod[:], four.unsqueeze(2).to_broadcast([P, 4, EX, GH]),
                                       gw2.unsqueeze(1).to_broadcast([P, 4, EX, GH]), ALU.mult))
                step(dve.tensor_reduce(gates[:, 4 * q:4 * q + 4, :], prod[:], AX.X, ALU.add))
            step(dve.tensor_tensor(gates[:], gates[:], row(gb2, EX), ALU.add))
            for k, top in enumerate((top1, top2)):
                step(dve.tensor_reduce(top, gates[:], AX.X, ALU.max))
                step(dve.tensor_tensor(cand[:], gates[:], wide(top, EX), ALU.is_equal))
                step(dve.tensor_tensor(cand[:], cand[:], row(rank, EX), ALU.mult))
                step(dve.tensor_reduce(inv, cand[:], AX.X, ALU.max))
                step(dve.tensor_tensor(hot[:, k, :, :], cand[:], wide(inv, EX), ALU.is_equal))
                if k == 0:
                    step(dve.scalar_tensor_tensor(out=gates[:], in0=hot[:, 0, :, :], scalar=-3e38, in1=gates[:],
                                                  op0=ALU.mult, op1=ALU.add))
            for k in range(2):
                last = dve.tensor_reduce(cnt[:, k, :], hot[:, k, :, :].rearrange("p n e -> p e n"), AX.X, ALU.add)
            last.then_inc(cnt_hot, 1)
            step(dve.tensor_tensor(gap, top2, top1, ALU.subtract))
            assert steps[0] == GATE_GAP
            dve.wait_ge(gate_act, 2)
            step(dve.tensor_scalar(inv, gap, 1.0, None, ALU.add))
            step(dve.reciprocal(top1, inv))
            step(dve.tensor_scalar(top1, top1, 1.0 / R, None, ALU.mult))
            step(dve.tensor_tensor(top2, top1, gap, ALU.mult))
            dve.wait_ge(cnt_psum, 1)
            step(dve.tensor_scalar(allow[:], bank6[:, 256:256 + 2 * EX].rearrange("p (k e) -> p k e", k=2),
                                   float(CAPACITY), None, ALU.is_le))
            for k, top in enumerate((top1, top2)):
                step(dve.tensor_tensor(hot[:, k, :, :], hot[:, k, :, :], wide(top, EX), ALU.mult))
                step(dve.tensor_tensor(hot[:, k, :, :], hot[:, k, :, :], row(allow[:, k, :], EX), ALU.mult))
            dve.tensor_tensor(wmix[:], hot[:, 0, :, :], hot[:, 1, :, :], ALU.add).then_inc(wmix_ready, 1)

            with dve.Fori(0, PAIRS // 2) as i:
                for u in range(2):
                    n = 2 * i + u
                    dve.wait_ge(lb_psum, n + 1)
                    dve.tensor_tensor(acc[:, bass.ds(n, 1), :], slot[u][:].unsqueeze(1), acc[:, bass.ds(n, 1), :],
                                      ALU.add).then_inc(out_ready, 1)


def _phased(a):
    return a.reshape(*a.shape[:-1], LP, PH).swapaxes(-1, -2).reshape(a.shape)


def _layout(i):
    x = np.asarray(i["x"], np.float32)
    rows = x.reshape(PAIRS, P, L)
    a = {}
    a["xt"] = rows.reshape(PAIRS, P, KC, P).transpose(0, 3, 2, 1)
    a["xp"] = _phased(rows)
    a["emb_t"] = i["cond_128"].T
    a["c_w0"] = i["L0_cond_W0"]
    a["c_b0"] = i["L0_cond_b0"].reshape(P, 1)
    a["c_w1"] = i["L0_cond_W1"]
    a["c_b1"] = i["L0_cond_b1"].reshape(P, 1)
    a["c_w2"] = i["L0_cond_W2"]
    a["c_b2"] = np.tile(i["L0_cond_b2"], (BS, 1))
    a["c_w"] = i["L0_cond_weight"][..., 0].transpose(0, 2, 1).reshape(EX, CH * CH)
    a["c_bk"] = np.stack([i["L0_cond_bias_k"]] * 2, 1)
    wqkv = i["L0_attn_Wqkv"].reshape(KC, P, QKV)
    a["wq"] = wqkv[:, :, :L]
    a["wkv"] = wqkv[:, :, L:].transpose(1, 0, 2)
    a["wo"] = _phased(i["L0_attn_Wo"]).reshape(KC, P, L)
    slopes = ((2.0 ** -0.25) ** np.arange(1, NH + 1, dtype=np.float64)).astype(np.float32)
    q, k = np.arange(CH)[:, None, None], np.arange(CH)[None, None, :]
    tab = np.where(k <= q, slopes[None, :, None] * (k - q).astype(np.float32), np.float32(NEG))
    a["tab"] = np.concatenate([tab, tab]).astype(np.float32)
    a["ident_d"] = np.eye(P, dtype=np.float32)
    w = i["L0_cond2_weight"]
    cw = np.zeros((PH, 32, 2, 3, PH, 32), np.float32)
    for s in range(3):
        for qi in range(PH):
            for po in range(PH):
                t = 4 * (s - 1) + qi - po + TAPS // 2
                if 0 <= t < TAPS:
                    for g in range(4):
                        at = 16 * (g % 2)
                        cw[qi, at:at + 16, g // 2, s, po, at:at + 16] = w[16 * g:16 * g + 16, :, t].T
    a["conv_w"] = cw.reshape(P, 2, 3, P)
    a["cw_t"] = i["L0_cond2_c_weight"].T
    a["fside"] = i["fside_S_0"].reshape(1, CH)

    def in_rows(m):
        return m.reshape(2, P, PH, -1).transpose(1, 0, 2, 3).reshape(P, KC, -1)

    a["ffn_w"] = in_rows(_phased(i["L0_ffn_weight"].T)).transpose(1, 0, 2)
    lora_a = i["L0_ffn_lora_A"].transpose(1, 0, 2).reshape(L, EX * R)
    a["lg_w"] = in_rows(np.concatenate([lora_a, i["L0_ffn_gw1"].T], 1))
    a["lora_b"] = _phased(i["L0_ffn_lora_B"].reshape(EX * R, L))
    a["gate_c"] = np.tile(np.concatenate([i["L0_ffn_gb1"], i["L0_ffn_ln_gamma"], i["L0_ffn_ln_beta"],
                                          i["L0_ffn_gw2"].reshape(-1), i["L0_ffn_gb2"],
                                          np.arange(EX, 0, -1).astype(np.float32)]), (P, 1))
    return {k: np.ascontiguousarray(v) for k, v in a.items()}


def kernel(**inputs):
    import concourse.bacc as _bacc
    from concourse.bass_utils import run_bass_kernel_spmd as _run

    host = _layout({k: np.asarray(v) for k, v in inputs.items()})
    nc = _bacc.Bacc("TRN2", target_bir_lowering=False, num_devices=1)
    arrays, args = {}, {}
    for name, a in host.items():
        arrays[f"in_{name}"] = a
        args[name] = nc.dram_tensor(f"in_{name}", a.shape, mybir.dt.from_np(a.dtype), kind="ExternalInput").ap()
    out = nc.dram_tensor("out_0", (PAIRS, P, L), F32, kind="ExternalOutput").ap()
    build(nc, out=out, **args)
    r = _run(nc, [arrays], core_ids=[0]).results[0]["out_0"]
    return np.ascontiguousarray(r.reshape(BS * CH, PH, LP).swapaxes(1, 2)).reshape(BS, CH, L)
```

```python
from contextlib import ExitStack

import numpy as np

import concourse.bass as bass
from concourse import mybir

F32 = mybir.dt.float32
F32R = mybir.dt.float32r
ALU = mybir.AluOpType
ACT = mybir.ActivationFunctionType
AX = mybir.AxisListType

P = 128
BS, CH, L = 32, 64, 1024
PAIRS = BS // 2
KC = L // P
NH, HD = 32, 32
QKV = NH * HD + 2 * HD
EX = 8
R = 16
GH = 4 * EX
LG = EX * R + GH
TAPS, PH = 9, 4
LP = L // PH
N_TOK = BS * CH
CAPACITY = int(3.0 * N_TOK / EX)
HALF = 1024
NEG = -1e30
N_COND = 10
COND_ATT = 4
COND_ROWS = 8
COND_AGG = 5
GATE_VAR = 7
GATE_GAP = 24
GATE_STEPS = 29



def wait_past(eng, semaphore, value):
    if not isinstance(value, int) or value > 0:
        eng.wait_ge(semaphore, value)


def build(nc, xt, xp, emb_t, c_w0, c_b0, c_w1, c_b1, c_w2, c_b2, c_w, c_bk, wq, wkv, wo, tab, ident_d,
          conv_w, cw_t, fside, ffn_w, lg_w, lora_b, gate_c, out):
    agg_d = nc.dram_tensor("agg_d", (BS, CH, CH), F32, kind="Internal").ap()
    aggb_d = nc.dram_tensor("aggb_d", (PAIRS, P), F32, kind="Internal").ap()
    ctxb_d = nc.dram_tensor("ctxb_d", (PAIRS, P), F32, kind="Internal").ap()
    x1_d = nc.dram_tensor("x1_d", (PAIRS, P, L), F32, kind="Internal").ap()

    ctx = ExitStack()
    with ctx:
        def sb(name, shape, dt=F32, stack=ctx):
            return stack.enter_context(nc.sbuf_tensor(name, shape, dt))

        def sem(name):
            return ctx.enter_context(nc.semaphore(name))

        w_hi = sb("w_hi", [P, KC, L], F32R)
        w_lo = sb("w_lo", [P, KC, L], F32R)
        stage = sb("stage", [P, 2, L])
        ident = sb("ident", [P, P])
        wc = sb("wc", [P, 2, 3, P])

        a_mem = ExitStack()
        early = ExitStack()
        cw_sb = sb("cw_sb", [EX, CH * CH], F32, early)
        agg_sb = sb("agg_sb", [BS, CH * CH], F32, early)
        early.close()
        wo_hi = sb("wo_hi", [P, KC, L], F32R, a_mem)
        wo_lo = sb("wo_lo", [P, KC, L], F32R, a_mem)
        x_hi = sb("x_hi", [P, KC, P], F32R, a_mem)
        x_lo = sb("x_lo", [P, KC, P], F32R, a_mem)
        tab_sb = sb("tab_sb", [P, NH, CH], F32, a_mem)
        sc = sb("sc", [P, NH, CH], F32, a_mem)
        pt = sb("pt", [P, NH // 2, P], F32, a_mem)
        qt = sb("qt", [P, KC, P], F32, a_mem)
        xt_sb = sb("xt_sb", [P, KC, P], F32, a_mem)
        y = sb("y", [P, L], F32, a_mem)
        wkv_sb = sb("wkv_sb", [P, KC, 2 * HD], F32, a_mem)
        bdk = sb("bdk", [P, 2, 4, CH], F32, a_mem)
        bdagg = sb("bdagg", [P, 2, 2, CH], F32, a_mem)
        bdv = sb("bdv", [P, 2, 2 * HD], F32, a_mem)
        aggb = sb("aggb", [P, P], F32, a_mem)
        yk4 = sb("yk4", [P, 4, HD], F32, a_mem)
        yv = sb("yv", [P, HD], F32, a_mem)
        ones = sb("ones", [P, P], F32, a_mem)
        cs_q = sb("cs_q", [P, KC + 1], F32, a_mem)
        cs_v = sb("cs_v", [P, HD], F32, a_mem)
        aggb_c = sb("aggb_c", [P, BS], F32, a_mem)
        aggb_p = sb("aggb_p", [P, 2], F32, a_mem)
        mx = sb("mx", [P, NH], F32, a_mem)
        sm = sb("sm", [P, NH], F32, a_mem)
        rs = sb("rs", [P, NH], F32, a_mem)
        b01_sb = sb("b01_sb", [P, 2], F32, a_mem)
        w2_sb = sb("w2_sb", [P, EX], F32, a_mem)
        b2_sb = sb("b2_sb", [BS, EX], F32, a_mem)
        bk_sb = sb("bk_sb", [EX, 2, CH], F32, a_mem)
        fs_sb = sb("fs_sb", [1, CH], F32, a_mem)
        h_sb = sb("h_sb", [P, 2, BS], F32, a_mem)
        att = sb("att", [BS, EX], F32, a_mem)
        att_s = sb("att_s", [BS, 3], F32, a_mem)
        att_t = sb("att_t", [EX, BS], F32, a_mem)
        rows = sb("rows", [BS, 2, CH], F32, a_mem)
        early = ExitStack()
        wsum = sb("wsum", [P, QKV], F32, early)
        wsumk4 = sb("wsumk4", [P, 4, HD], F32, early)
        emb_sb = sb("emb_sb", [P, BS], F32, early)
        cwt_sb = sb("cwt_sb", [P, CH], F32, early)
        w0_sb = sb("w0_sb", [P, P], F32, early)
        w1_sb = sb("w1_sb", [P, P], F32, early)
        early.close()
        at_hi = sb("at_hi", [P, KC, P], F32R, a_mem)
        at_lo = sb("at_lo", [P, KC, P], F32R, a_mem)
        xres = sb("xres", [P, L], F32, a_mem)
        a_mem.close()

        acc = sb("acc", [P, PAIRS, L])
        x4 = sb("x4", [P, 4, LP + 2])
        ctxb = sb("ctxb", [P, P])
        cv = sb("cv", [P, 2, KC, P])
        cv_hi = sb("cv_hi", [P, 2, KC, P], F32R)
        cv_lo = sb("cv_lo", [P, 2, KC, P], F32R)
        lgw = sb("lgw", [P, KC, LG])
        x1r = sb("x1r", [P, L])
        tmp_a = sb("tmp_a", [P, PAIRS, EX * R])
        gc = sb("gc", [P, 3 * GH + EX * GH + 2 * EX])
        g_in = sb("g_in", [P, GH])
        g_h = sb("g_h", [P, GH])
        g_sq = sb("g_sq", [P, GH])
        g_prod = sb("g_prod", [P, EX, GH])
        g_s = sb("g_s", [P, 8])
        gates = sb("gates", [P, EX])
        cand = sb("cand", [P, EX])
        hot1 = sb("hot1", [P, 2, EX])
        lb_sb = sb("lb_sb", [P, L])
        hot = sb("hot", [P, 2, PAIRS, EX])
        whot = sb("whot", [P, 2, PAIRS, EX])
        cnt = sb("cnt", [P, 2, EX])
        allow = sb("allow", [P, 2, EX])
        wmix = sb("wmix", [P, PAIRS, EX])
        ones_c = sb("ones_c", [P, P])
        tmpw = sb("tmpw", [P, 2, EX * R])
        tt_sb = sb("tt_sb", [P, 2, P])

        rows3 = "p a b -> p (a b)"
        places = [stage[:, 0, :], stage[:, 1, :], sc[:, 0:16, :].rearrange(rows3), sc[:, 16:32, :].rearrange(rows3),
                  pt[:, 0:8, :].rearrange(rows3), pt[:, 8:16, :].rearrange(rows3), xres[:],
                  xt_sb[:].rearrange(rows3), y[:]]
        PLACE = [0, 1, 2, 3, 4, 5, 0, 1] + [6, 0, 1, 6, 0, 1, 6, 0] + [1, 0, 7, 8, 1, 0, 7, 8]

        def before_in_place(n):
            return max((m for m in range(n) if PLACE[m] == PLACE[n]), default=None)

        def landed(eng, n):
            eng.wait_ge(ld_stage[PLACE[n]], 16 * (PLACE[:n + 1].count(PLACE[n])))

        slot = [ctx.enter_context(nc.psum_tensor(f"slot{i}", [P, HALF], F32)) for i in range(3)]
        bank6 = ctx.enter_context(nc.psum_tensor("bank6", [P, 512], F32))
        bank7 = ctx.enter_context(nc.psum_tensor("bank7", [P, 512], F32))

        ld_cond, ld_const, ld_late = sem("ld_cond"), sem("ld_const"), sem("ld_late")
        ld_wkv = sem("ld_wkv")
        ld_stage = [sem(f"ld_stage{k}") for k in range(len(places))]
        ld_xt, ld_agg, ld_aggb, ld_xres = sem("ld_xt"), sem("ld_agg"), sem("ld_aggb"), sem("ld_xres")
        st_rows, st_x1 = sem("st_rows"), sem("st_x1")
        zeroed, cond_pe, cond_act, cond_dve = sem("zeroed"), sem("cond_pe"), sem("cond_act"), sem("cond_dve")
        agg_act, agg_dve = sem("agg_act"), sem("agg_dve")
        w_hi_done, w_lo_done, w_sum_done = sem("w_hi_done"), sem("w_lo_done"), sem("w_sum_done")
        wsum_kv, cs_psum, cs_ready = sem("wsum_kv"), sem("cs_psum"), sem("cs_ready")
        x_hi_ready, x_lo_ready, y_psum, y_ready = sem("x_hi_ready"), sem("x_lo_ready"), sem("y_psum"), sem("y_ready")
        qt_psum, qt_ready, vv_psum = sem("qt_psum"), sem("qt_ready"), sem("vv_psum")
        aggb_picked, bdv_ready = sem("aggb_picked"), sem("bdv_ready")
        score_psum, score_ready, max_ready = sem("score_psum"), sem("score_ready"), sem("max_ready")
        shifted, exp_ready, sum_ready = sem("shifted"), sem("exp_ready"), sem("sum_ready")
        rsum_ready, prob_ready, pt_psum, pt_ready = sem("rsum_ready"), sem("prob_ready"), sem("pt_psum"), sem("pt_ready")
        at_psum, at_hi_ready, at_lo_ready = sem("at_psum"), sem("at_hi_ready"), sem("at_lo_ready")
        wo_psum, x1_ready = sem("wo_psum"), sem("x1_ready")
        ld_b, ld_x4, ld_ctx, ld_x1r, st_out = sem("ld_b"), sem("ld_x4"), sem("ld_ctx"), sem("ld_x1r"), sem("st_out")
        pads_zero, conv_psum, cv_ready = sem("pads_zero"), sem("conv_psum"), sem("cv_ready")
        cv_hi_ready, cv_lo_ready, lg_psum, lg_ready = sem("cv_hi_ready"), sem("cv_lo_ready"), sem("lg_psum"), sem("lg_ready")
        main_psum, acc_ready = sem("main_psum"), sem("acc_ready")
        gate_dve, gate_act, cnt_hot, cnt_psum, wmix_ready = sem("gate_dve"), sem("gate_act"), sem("cnt_hot"), sem("cnt_psum"), sem("wmix_ready")
        routed = sem("routed")
        tmpw_ready, tt_psum, tt_ready, lb_psum, out_ready = sem("tmpw_ready"), sem("tt_psum"), sem("tt_ready"), sem("lb_psum"), sem("out_ready")

        LAST = PAIRS - 1
        flat = "p a b -> p (a b)"
        block = ctx.enter_context(nc.Block())

        @block.sync
        def _(sp):
            sp.dma_start(xt_sb[:], xt[0]).then_inc(ld_xt, 16)
            conds = ((emb_sb[:], emb_t), (w0_sb[:], c_w0), (b01_sb[:, 0:1], c_b0), (w1_sb[:], c_w1),
                     (b01_sb[:, 1:2], c_b1), (w2_sb[:], c_w2), (b2_sb[:], c_b2), (bk_sb[:], c_bk),
                     (cwt_sb[:], cw_t), (fs_sb[:], fside))
            assert len(conds) == N_COND
            for t, s in conds:
                sp.dma_start(t, s).then_inc(ld_cond, 16)
            sp.dma_start(ident[:], ident_d).then_inc(ld_const, 16)
            sp.dma_start(cw_sb[:], c_w).then_inc(ld_const, 16)

            def stage_in(n, src):
                m = before_in_place(n)
                if m is not None:
                    sp.wait_ge(w_hi_done, m + 1)
                    sp.wait_ge(w_lo_done, m + 1)
                    if m < KC:
                        sp.wait_ge(w_sum_done, m + 1)
                sp.dma_start(places[PLACE[n]], src).then_inc(ld_stage[PLACE[n]], 16)

            for c in range(KC):
                stage_in(c, wq[c])
            sp.dma_start(wkv_sb[:], wkv).then_inc(ld_wkv, 16)
            sp.wait_ge(agg_act, 2)
            sp.wait_ge(agg_dve, 2)
            sp.dma_start(agg_d.rearrange("b i o -> b (i o)"), agg_sb[:]).then_inc(st_rows, 16)
            sp.wait_ge(cond_dve, COND_ROWS)
            sp.dma_start(aggb_d.rearrange("n (b o) -> (n b) o", b=2), rows[:, 0, :]).then_inc(st_rows, 16)
            sp.dma_start(ctxb_d.rearrange("n (b o) -> (n b) o", b=2), rows[:, 1, :]).then_inc(st_rows, 16)
            sp.wait_ge(st_rows, 48)
            sp.wait_ge(zeroed, 4)

            def load_agg(n):
                for b in range(2):
                    for r in range(2):
                        sp.dma_start(bdagg[CH * b:CH * b + CH, b, r, :], agg_d[2 * n + b]).then_inc(ld_agg, 16)
                sp.dma_start(aggb[:], aggb_d[n].partition_broadcast(P)).then_inc(ld_aggb, 16)

            load_agg(0)
            for c in range(3):
                stage_in(KC + c, wo[c])
            sp.dma_start(tab_sb[:], tab).then_inc(ld_late, 16)
            sp.dma_start(wc[:], conv_w).then_inc(ld_late, 16)

            def next_x(n):
                sp.wait_ge(y_psum, n)
                sp.dma_start(xt_sb[:], xt[n]).then_inc(ld_xt, 16)

            def next_agg(n):
                sp.wait_ge(vv_psum, n)
                sp.wait_ge(qt_ready, n)
                load_agg(n)

            def residual(n):
                wait_past(sp, st_x1, 16 * n)
                sp.dma_start(xres[:], xp[n]).then_inc(ld_xres, 16)

            def store_x1(n):
                sp.wait_ge(x1_ready, n + 1)
                sp.dma_start(x1_d[n], xres[:]).then_inc(st_x1, 16)

            next_x(1)
            next_agg(1)
            for c in range(3, KC):
                stage_in(KC + c, wo[c])
            next_x(2)
            sp.wait_ge(w_hi_done, 2 * KC)
            sp.wait_ge(w_lo_done, 2 * KC)

            def a_loads(i):
                next_agg(i + 1)
                residual(i - 1)
                next_x(i + 2)
                store_x1(i - 1)

            a_loads(1)
            with sp.Fori(2, LAST - 1) as i:
                a_loads(i)

            next_agg(LAST)
            residual(LAST - 2)
            for c in range(4):
                if c == 2:
                    sp.wait_ge(y_psum, PAIRS)
                if c == 3:
                    sp.wait_ge(qt_psum, PAIRS)
                stage_in(2 * KC + c, ffn_w[c])
            store_x1(LAST - 2)
            residual(LAST - 1)

            def load_x4(n):
                for ph in range(PH):
                    sp.dma_start(x4[32 * ph:32 * ph + 32, :, 1:LP + 1],
                                 x1_d[n][:, LP * ph:LP * ph + LP].rearrange("(g c) l -> c g l", g=4)
                                 ).then_inc(ld_x4, 16)

            def load_ctx(n):
                sp.dma_start(ctxb[:], ctxb_d[n].partition_broadcast(P)).then_inc(ld_ctx, 16)

            sp.wait_ge(pads_zero, 1)
            load_x4(0)
            load_ctx(0)
            for c in range(4, KC):
                stage_in(2 * KC + c, ffn_w[c])
            store_x1(LAST - 1)
            residual(LAST)
            sp.wait_ge(conv_psum, 1)
            sp.dma_start(lgw[:], lg_w).then_inc(ld_b, 16)
            sp.dma_start(gc[:], gate_c).then_inc(ld_b, 16)
            sp.dma_start(x1r[:], x1_d[0]).then_inc(ld_x1r, 16)
            sp.wait_ge(st_x1, 32)
            load_x4(1)
            sp.wait_ge(cv_ready, 1)
            load_ctx(1)
            store_x1(LAST)
            sp.wait_ge(st_x1, 16 * PAIRS)
            sp.dma_start(lb_sb[:], lora_b).then_inc(ld_b, 16)

            def b_next(n):
                sp.wait_ge(conv_psum, n)
                load_x4(n)
                sp.wait_ge(cv_ready, n)
                load_ctx(n)

            def b_residual(n):
                sp.wait_ge(acc_ready, n)
                sp.dma_start(x1r[:], x1_d[n]).then_inc(ld_x1r, 16)

            with sp.Fori(1, LAST) as i:
                b_next(i + 1)
                b_residual(i)
            b_residual(LAST)

            with sp.Fori(0, PAIRS) as i:
                sp.wait_ge(out_ready, i + 1)
                sp.dma_start(out[i], acc[:, bass.ds(i, 1), :].rearrange("p a n -> p (a n)")).then_inc(st_out, 16)
            sp.wait_ge(st_out, 16 * PAIRS)

        @block.tensor
        def _(pe):
            def split_product(dst, a_hi, a_lo, b_hi, b_lo, before=lambda c: None):
                for c in range(KC):
                    before(c)
                    for t, (a, b) in enumerate(((a_hi, b_hi), (a_hi, b_lo), (a_lo, b_hi))):
                        for k in range(2):
                            m = pe.matmul(dst[:, 512 * k:512 * k + 512], a(c), b[:, c, 512 * k:512 * k + 512],
                                          start=(c == 0 and t == 0), stop=(c == KC - 1 and t == 2))
                return m

            pe.wait_ge(ld_cond, 16 * N_COND)
            pe.matmul(bank7[:, 0:BS], w0_sb[:], emb_sb[:], start=True, stop=True).then_inc(cond_pe, 1)
            pe.wait_ge(cond_act, 1)
            pe.matmul(bank7[:, BS:2 * BS], w1_sb[:], h_sb[:, 0, :], start=True, stop=True).then_inc(cond_pe, 1)
            pe.wait_ge(cond_act, 2)
            pe.matmul(bank7[0:BS, 64:64 + EX], h_sb[:, 1, :], w2_sb[:], start=True, stop=True).then_inc(cond_pe, 1)
            pe.wait_ge(cond_dve, COND_ATT)
            pe.wait_ge(ld_const, 32)
            pe.transpose(bank7[0:EX, 128:128 + BS], att[:], ident[0:BS, 0:BS]).then_inc(cond_pe, 1)
            pe.wait_ge(cond_dve, COND_ATT + 1)
            pe.wait_ge(zeroed, 4)
            pe.matmul(bank7[0:BS, 192:192 + CH], att_t[:], bk_sb[:, 0, :], start=True, stop=True)
            pe.matmul(bank7[:, 256:256 + BS], bk_sb[:, :, :].rearrange(flat), att_t[:], start=True, stop=True)
            pe.matmul(bank7[0:BS, 320:320 + CH], ones[0:1, 0:BS], fs_sb[:], start=True, stop=False)
            pe.matmul(bank7[0:BS, 320:320 + CH], emb_sb[:], cwt_sb[:], start=False, stop=True).then_inc(cond_pe, 1)
            for g in range(4):
                if g == 3:
                    pe.wait_ge(agg_act, 1)
                for k in range(2):
                    at = HALF * g + 512 * k
                    m = pe.matmul(slot[g % 3][0:BS, 512 * k:512 * k + 512], att_t[:], cw_sb[:, at:at + 512],
                                  start=True, stop=True)
                m.then_inc(cond_pe, 1)

            def products(n, before=lambda c: None):
                pe.wait_ge(x_hi_ready, n + 1)
                pe.wait_ge(x_lo_ready, n + 1)
                split_product(slot[2], lambda c: x_hi[:, c, :], lambda c: x_lo[:, c, :], w_hi, w_lo, before)
                for c in range(KC):
                    m = pe.matmul(bank6[:, 0:2 * HD], xt_sb[:, c, :], wkv_sb[:, c, :],
                                  start=(c == 0), stop=(c == KC - 1))
                m.then_inc(y_psum, 1)

            def mix_q(n):
                pe.wait_ge(y_ready, n + 1)
                pe.wait_ge(ld_agg, 64 * (n + 1))
                for c in range(KC):
                    pe.matmul(slot[2][:, P * c:P * c + P].rearrange("p (b o) -> p b o", b=2),
                              y[:, P * c:P * c + P], bdagg[:, :, 0, :], start=True, stop=True)
                pe.matmul(bank6[:, P:2 * P].rearrange("p (b o) -> p b o", b=2), yk4[:, :, :].rearrange(flat),
                          bdagg[:, :, 0, :], start=True, stop=True).then_inc(qt_psum, 1)

            def mix_v(n):
                for b in range(2):
                    m = pe.matmul(bank7[:, HD * b:HD * b + HD], bdagg[:, b, :, :].rearrange(flat), yv[:],
                                  start=True, stop=True)
                m.then_inc(vv_psum, 1)

            def scores(i):
                pe.wait_ge(qt_ready, i + 1)
                for hh in range(2):
                    for c in range(4):
                        for b in range(2):
                            m = pe.matmul(slot[hh][CH * b:CH * b + CH, 256 * c:256 * c + 256],
                                          qt[:, 4 * hh + c, CH * b:CH * b + CH],
                                          bdk[:, b, :, :].rearrange(flat), start=True, stop=True)
                    m.then_inc(score_psum, 1)

            def turn_probs(i):
                for hh in range(2):
                    pe.wait_ge(prob_ready, 2 * i + hh + 1)
                    for k in range(8):
                        h = 16 * hh + 2 * k
                        m = pe.transpose(slot[hh][:, P * k:P * k + P], sc[:, h:h + 2, :].rearrange(flat), ident[:])
                    m.then_inc(pt_psum, 1)

            def attend(i):
                pe.wait_ge(pt_ready, 2 * i + 2)
                pe.wait_ge(bdv_ready, i + 1)
                for b in range(2):
                    for eo in range(2):
                        m = pe.matmul(slot[2][CH * eo:CH * eo + CH, 512 * b:512 * b + 512]
                                      .rearrange("p (c t) -> p c t", c=KC), bdv[:, b, :],
                                      pt[:, eo::2, CH * b:CH * b + CH], start=True, stop=True)
                m.then_inc(at_psum, 1)

            def project(n):
                pe.wait_ge(at_hi_ready, n + 1)
                pe.wait_ge(at_lo_ready, n + 1)
                split_product(slot[1], lambda c: at_hi[:, c, :], lambda c: at_lo[:, c, :], wo_hi, wo_lo
                              ).then_inc(wo_psum, 1)

            def chunk_split(c):
                pe.wait_ge(w_hi_done, c + 1)
                pe.wait_ge(w_lo_done, c + 1)

            pe.wait_ge(agg_act, 2)
            pe.wait_ge(ld_wkv, 16)
            products(0, chunk_split)
            pe.wait_ge(wsum_kv, 2)
            pe.wait_ge(w_sum_done, KC)
            pe.wait_ge(cond_dve, COND_ROWS)
            for c in range(KC):
                pe.matmul(bank7[:, 128 + c:129 + c], wsum[:, P * c:P * c + P], ones[:, 0:1], start=True, stop=True)
            pe.matmul(bank7[:, 136:137], wsumk4[:, :, :].rearrange(flat), ones[:, 0:1], start=True, stop=True)
            pe.matmul(bank7[:, 160:160 + HD], ones[:], wsum[:, L + HD:QKV], start=True, stop=True
                      ).then_inc(cs_psum, 1)
            mix_q(0)
            pe.wait_ge(cs_ready, 2)
            mix_v(0)

            def pair(i, first=False):
                wait_past(pe, x1_ready, i - 1)
                scores(i)
                wait_past(pe, at_lo_ready, i)
                products(i + 1)
                turn_probs(i)
                mix_q(i + 1)
                if not first:
                    pe.wait_ge(pt_ready, 2 * i + 2)
                    project(i - 1)
                pe.wait_ge(qt_ready, i + 2)
                attend(i)
                mix_v(i + 1)

            pe.wait_ge(agg_dve, 2)
            pair(0, True)
            chunk_split(2 * KC - 1)
            pair(1)
            with pe.Fori(2, LAST) as i:
                pair(i)
            pe.wait_ge(x1_ready, LAST - 1)
            scores(LAST)
            pe.wait_ge(score_ready, 2 * PAIRS)
            project(LAST - 1)
            pe.wait_ge(x1_ready, LAST)
            turn_probs(LAST)
            pe.wait_ge(at_lo_ready, LAST)
            attend(LAST)

            def conv(n):
                pe.wait_ge(ld_x4, 64 * (n + 1))
                for g in range(4):
                    for j in range(2):
                        for s in range(3):
                            m = pe.matmul(slot[0][:, 512 * j:512 * j + 512].rearrange("p (a t) -> p a t", a=PH)
                                          [:, :, 32 * g:32 * g + 32],
                                          x4[:, g, P * j + s:P * j + s + P], wc[:, g % 2, s, :],
                                          start=(s == 0), stop=(s == 2))
                m.then_inc(conv_psum, 1)

            def gate_and_lora(n, u):
                pe.wait_ge(cv_ready, n + 1)
                wait_past(pe, lg_ready, n)
                for c in range(KC):
                    m = pe.matmul(bank6[:, 0:LG], cv[:, u, c, :], lgw[:, c, :], start=(c == 0), stop=(c == KC - 1))
                m.then_inc(lg_psum, 1)

            def dense(n, u):
                pe.wait_ge(cv_hi_ready, n + 1)
                pe.wait_ge(cv_lo_ready, n + 1)
                wait_past(pe, acc_ready, n)
                split_product(slot[1], lambda c: cv_hi[:, u, c, :], lambda c: cv_lo[:, u, c, :], w_hi, w_lo
                              ).then_inc(main_psum, 1)

            pe.wait_ge(ld_late, 32)
            conv(0)
            project(LAST)
            chunk_split(3 * KC - 1)
            pe.wait_ge(ld_b, 32)

            def two_pairs(i):
                for u in range(2):
                    pe.wait_ge(cv_ready, 2 * i + u + 1)
                    conv(2 * i + u + 1)
                    gate_and_lora(2 * i + u, u)
                    dense(2 * i + u, u)

            pe.wait_ge(x1_ready, PAIRS)
            two_pairs(0)
            with pe.Fori(1, PAIRS // 2 - 1) as i:
                two_pairs(i)
            pe.wait_ge(cv_ready, LAST)
            conv(LAST)
            gate_and_lora(LAST - 1, 0)
            gate_and_lora(LAST, 1)
            dense(LAST - 1, 0)
            dense(LAST, 1)

            pe.wait_ge(cnt_hot, 1)
            pe.wait_ge(lg_ready, PAIRS)
            pe.matmul(bank6[:, 256:256 + 2 * EX], ones_c[:], cnt[:, :, :].rearrange(flat), start=True, stop=True
                      ).then_inc(cnt_psum, 1)
            turned = [bank6, bank7]

            def lora(i, first=False):
                for u in range(2):
                    pe.wait_ge(tmpw_ready, 2 * i + u + 1)
                    pe.transpose(turned[u][:, 0:P], tmpw[:, u, :], ident[:]).then_inc(tt_psum, 1)
                for u in range(2):
                    n = 2 * i + u
                    pe.wait_ge(tt_ready, n + 1)
                    if not first:
                        pe.wait_ge(out_ready, n - 1)
                    for k in range(2):
                        m = pe.matmul(slot[u][:, 512 * k:512 * k + 512], tt_sb[:, u, :],
                                      lb_sb[:, 512 * k:512 * k + 512], start=True, stop=True)
                    m.then_inc(lb_psum, 1)

            pe.wait_ge(acc_ready, PAIRS)
            pe.wait_ge(ld_b, 48)
            lora(0, True)
            with pe.Fori(1, PAIRS // 2) as i:
                lora(i)

        @block.scalar
        def _(act):
            act.wait_ge(ld_xt, 16)
            act.activation(x_hi[:], xt_sb[:], ACT.Copy).then_inc(x_hi_ready, 1)
            act.wait_ge(ld_cond, 16 * N_COND)
            for t in range(2):
                act.wait_ge(cond_pe, t + 1)
                act.activation(h_sb[:, t, :], bank7[:, BS * t:BS * t + BS], ACT.Gelu, bias=b01_sb[:, t:t + 1]
                               ).then_inc(cond_act, 1)
            act.wait_ge(cond_dve, 2)
            act.activation(att[:], att[:], ACT.Exp, bias=att_s[:, 0:1], accum_out=att_s[:, 1:2]).then_inc(cond_act, 1)

            def split_hi(n, dst, c):
                landed(act, n)
                act.activation(dst[:, c, :], places[PLACE[n]], ACT.Copy).then_inc(w_hi_done, 1)

            def x_high(n):
                act.wait_ge(ld_xt, 16 * (n + 1))
                act.activation(x_hi[:], xt_sb[:], ACT.Copy).then_inc(x_hi_ready, 1)

            def y_copy(n):
                act.wait_ge(y_psum, n + 1)
                act.activation(y[:], slot[2][:], ACT.Copy)
                act.activation(yk4[:], bank6[:, 0:HD].unsqueeze(1).to_broadcast([P, 4, HD]), ACT.Copy)
                act.activation(yv[:], bank6[:, HD:2 * HD], ACT.Copy).then_inc(y_ready, 1)

            def exps(i):
                for hh in range(2):
                    act.wait_ge(shifted, 2 * i + hh + 1)
                    half = sc[:, 16 * hh:16 * hh + 16, :]
                    act.activation(half, half, ACT.Exp).then_inc(exp_ready, 1)

            def pt_copy(i):
                for hh in range(2):
                    act.wait_ge(pt_psum, 2 * i + hh + 1)
                    act.activation(pt[:, 8 * hh:8 * hh + 8, :], slot[hh][:].rearrange("p (h t) -> p h t", h=8),
                                   ACT.Copy).then_inc(pt_ready, 1)

            def at_high(i):
                act.wait_ge(at_psum, i + 1)
                act.activation(at_hi[:, :, :].rearrange("p c (b t) -> p b c t", b=2),
                               slot[2][:].rearrange("p (b c t) -> p b c t", b=2, c=KC), ACT.Copy
                               ).then_inc(at_hi_ready, 1)

            for c in range(2):
                split_hi(c, w_hi, c)
            for g in (0, 2):
                act.wait_ge(cond_pe, COND_AGG + g + 1)
                act.activation(agg_sb[:, HALF * g:HALF * g + HALF], slot[g % 3][0:BS, :], ACT.Copy
                               ).then_inc(agg_act, 1)
            for c in range(2, KC):
                split_hi(c, w_hi, c)
            y_copy(0)
            x_high(1)
            exps(0)
            act.wait_ge(st_rows, 48)
            for c in range(KC):
                split_hi(KC + c, wo_hi, c)
            y_copy(1)
            pt_copy(0)
            x_high(2)
            at_high(0)

            def pair(i):
                exps(i)
                y_copy(i + 1)
                pt_copy(i)
                x_high(i + 2)
                at_high(i)

            with act.Fori(1, LAST - 1) as i:
                pair(i)
            exps(LAST - 1)
            y_copy(LAST)
            pt_copy(LAST - 1)
            for c in range(4):
                split_hi(2 * KC + c, w_hi, c)
            at_high(LAST - 1)
            exps(LAST)
            for c in range(4, KC):
                split_hi(2 * KC + c, w_hi, c)
            pt_copy(LAST)
            at_high(LAST)

            def conv_high(n, u):
                act.wait_ge(cv_ready, n + 1)
                act.activation(cv_hi[:, u, :, :], cv[:, u, :, :], ACT.Copy).then_inc(cv_hi_ready, 1)

            def lg_copy(n):
                act.wait_ge(lg_psum, n + 1)
                wait_past(act, gate_dve, GATE_STEPS * n)
                act.activation(tmp_a[:, bass.ds(n, 1), :], bank6[:, 0:EX * R].unsqueeze(1), ACT.Copy)
                act.activation(g_in[:], bank6[:, EX * R:LG], ACT.Copy).then_inc(lg_ready, 1)

            def gate_parts(n):
                act.wait_ge(gate_dve, GATE_STEPS * n + GATE_VAR)
                act.activation(g_s[:, 2:3], g_s[:, 1:2], ACT.Sqrt).then_inc(gate_act, 1)
                act.wait_ge(gate_dve, GATE_STEPS * n + GATE_GAP)
                act.activation(g_s[:, 5:6], g_s[:, 4:5], ACT.Exp).then_inc(gate_act, 1)

            conv_high(0, 0)

            def two_pairs(i):
                for u in range(2):
                    lg_copy(2 * i + u)
                    wait_past(act, main_psum, 2 * i + u)
                    conv_high(2 * i + u + 1, 1 - u)
                    gate_parts(2 * i + u)

            two_pairs(0)
            with act.Fori(1, PAIRS // 2 - 1) as i:
                two_pairs(i)
            lg_copy(LAST - 1)
            act.wait_ge(main_psum, LAST - 1)
            conv_high(LAST, 1)
            gate_parts(LAST - 1)
            lg_copy(LAST)
            gate_parts(LAST)

            turned = [bank6, bank7]

            def turned_copy(i):
                for u in range(2):
                    act.wait_ge(tt_psum, 2 * i + u + 1)
                    wait_past(act, lb_psum, 2 * i)
                    act.activation(tt_sb[:, u, :], turned[u][:, 0:P], ACT.Copy).then_inc(tt_ready, 1)

            turned_copy(0)
            with act.Fori(1, PAIRS // 2) as i:
                turned_copy(i)

        @block.gpsimd
        def _(pool):
            for t, v in ((bdagg, 0.0), (bdk, 0.0), (bdv, 0.0), (ones, 1.0)):
                pool.memset(t[:], v).then_inc(zeroed, 1)

            def x_low(n):
                pool.wait_ge(x_hi_ready, n + 1)
                pool.tensor_tensor(x_lo[:], xt_sb[:], x_hi[:].bitcast(F32), ALU.subtract).then_inc(x_lo_ready, 1)

            x_low(0)
            for c in range(1, KC):
                landed(pool, c)
                if c == 1:
                    landed(pool, 0)
                    before = places[PLACE[0]]
                else:
                    pool.wait_ge(w_sum_done, c)
                    before = wsum[:, 0:L]
                pool.tensor_tensor(wsum[:, 0:L], before, places[PLACE[c]], ALU.add
                                   ).then_inc(w_sum_done, 2 if c == 1 else 1)
            pool.wait_ge(y_psum, 1)
            x_low(1)

            def shift_and_norm(i):
                for t, (ready, op, done) in enumerate(((max_ready, ALU.subtract, shifted), (rsum_ready, ALU.mult, prob_ready))):
                    v = (mx, rs)[t]
                    for hh in range(2):
                        pool.wait_ge(ready, 2 * i + hh + 1)
                        half = sc[:, 16 * hh:16 * hh + 16, :]
                        pool.tensor_tensor(half, half, v[:, 16 * hh:16 * hh + 16].unsqueeze(2)
                                           .to_broadcast([P, 16, CH]), op).then_inc(done, 1)

            with pool.Fori(0, LAST - 1) as i:
                shift_and_norm(i)
                x_low(i + 2)
            shift_and_norm(LAST - 1)
            shift_and_norm(LAST)

            def conv_low(n, u):
                pool.wait_ge(cv_hi_ready, n + 1)
                pool.tensor_tensor(cv_lo[:, u, :, :], cv[:, u, :, :], cv_hi[:, u, :, :].bitcast(F32), ALU.subtract
                                   ).then_inc(cv_lo_ready, 1)

            with pool.Fori(0, PAIRS // 2) as i:
                for u in range(2):
                    conv_low(2 * i + u, u)

            pool.wait_ge(wmix_ready, 1)
            pool.wait_ge(lg_ready, PAIRS)

            def weigh(n, u):
                pool.tensor_tensor(tmpw[:, u, :].rearrange("p (a e r) -> p a e r", a=1, r=R),
                                   tmp_a[:, bass.ds(n, 1), :].rearrange("p a (e r) -> p a e r", r=R),
                                   wmix[:, bass.ds(n, 1), :].unsqueeze(3).to_broadcast([P, 1, EX, R]), ALU.mult
                                   ).then_inc(tmpw_ready, 1)

            weigh(0, 0)
            weigh(1, 1)
            with pool.Fori(1, PAIRS // 2) as i:
                for u in range(2):
                    pool.wait_ge(tt_psum, 2 * i + u - 1)
                    weigh(2 * i + u, u)

        @block.vector
        def _(dve):
            def cond(ins, value):
                ins.then_inc(cond_dve, 1)
                dve.wait_ge(cond_dve, value)

            dve.wait_ge(cond_pe, 3)
            dve.wait_ge(ld_cond, 16 * N_COND)
            cond(dve.tensor_tensor(att[:], bank7[0:BS, 64:64 + EX], b2_sb[:], ALU.add), 1)
            cond(dve.tensor_reduce(att_s[:, 0:1], att[:], AX.X, ALU.max, negate=True), 2)
            dve.wait_ge(cond_act, 3)
            cond(dve.reciprocal(att_s[:, 2:3], att_s[:, 1:2]), 3)
            cond(dve.tensor_scalar(att[:], att[:], att_s[:, 2:3], None, ALU.mult), COND_ATT)
            dve.wait_ge(cond_pe, 4)
            cond(dve.tensor_copy(att_t[:], bank7[0:EX, 128:128 + BS]), COND_ATT + 1)
            dve.wait_ge(cond_pe, COND_AGG)
            dve.tensor_copy(rows[:, 0, :], bank7[0:BS, 192:192 + CH]).then_inc(cond_dve, 1)
            dve.tensor_copy(rows[:, 1, :], bank7[0:BS, 320:320 + CH]).then_inc(cond_dve, 1)
            dve.tensor_copy(aggb_c[:], bank7[:, 256:256 + BS]).then_inc(cond_dve, 1)

            def split_lo(n, dst_hi, dst_lo, c):
                dve.wait_ge(w_hi_done, n + 1)
                dve.tensor_tensor(dst_lo[:, c, :], places[PLACE[n]], dst_hi[:, c, :].bitcast(F32), ALU.subtract
                                  ).then_inc(w_lo_done, 1)

            split_lo(0, w_hi, w_lo, 0)
            split_lo(1, w_hi, w_lo, 1)
            for g in (1, 3):
                dve.wait_ge(cond_pe, COND_AGG + g + 1)
                dve.tensor_copy(agg_sb[:, HALF * g:HALF * g + HALF], slot[g % 3][0:BS, :]).then_inc(agg_dve, 1)
            for c in range(2, KC):
                split_lo(c, w_hi, w_lo, c)
            dve.wait_ge(ld_wkv, 16)
            dve.tensor_reduce(wsum[:, L:QKV], wkv_sb[:].rearrange("p c n -> p n c"), AX.X, ALU.add).then_inc(wsum_kv, 1)
            dve.wait_ge(wsum_kv, 1)
            dve.tensor_copy(wsumk4[:], wsum[:, L:L + HD].unsqueeze(1).to_broadcast([P, 4, HD])).then_inc(wsum_kv, 1)
            dve.wait_ge(cs_psum, 1)
            dve.tensor_copy(cs_q[:], bank7[:, 128:128 + KC + 1]).then_inc(cs_ready, 1)
            dve.tensor_copy(cs_v[:], bank7[:, 160:160 + HD]).then_inc(cs_ready, 1)
            dve.wait_ge(cs_ready, 2)

            def mixed_q(n):
                dve.wait_ge(qt_psum, n + 1)
                dve.wait_ge(ld_aggb, 16 * (n + 1))
                for c in range(KC):
                    dve.scalar_tensor_tensor(out=qt[:, c, :], in0=aggb[:], scalar=cs_q[:, c:c + 1],
                                             in1=slot[2][:, P * c:P * c + P], op0=ALU.mult, op1=ALU.add)
                for j in range(4):
                    q = slice(32 * j, 32 * j + 32)
                    last = dve.scalar_tensor_tensor(
                        out=bdk[q, :, j, :], in0=aggb[q, :].rearrange("p (b k) -> p b k", b=2),
                        scalar=cs_q[q, KC:KC + 1], in1=bank6[q, P:2 * P].rearrange("p (b k) -> p b k", b=2),
                        op0=ALU.mult, op1=ALU.add)
                last.then_inc(qt_ready, 1)

            def mixed_v(n):
                dve.wait_ge(vv_psum, n + 1)
                dve.tensor_copy(aggb_p[:], aggb_c[:, bass.ds(2 * n, 2)]).then_inc(aggb_picked, 1)
                dve.wait_ge(aggb_picked, n + 1)
                for b in range(2):
                    for r in range(2):
                        q = slice(CH * r, CH * r + CH)
                        last = dve.scalar_tensor_tensor(
                            out=bdv[q, b, HD * r:HD * r + HD], in0=cs_v[q, :], scalar=aggb_p[q, b:b + 1],
                            in1=bank7[q, HD * b:HD * b + HD], op0=ALU.mult, op1=ALU.add)
                last.then_inc(bdv_ready, 1)

            dve.wait_ge(zeroed, 4)
            dve.wait_ge(cond_dve, COND_ROWS)
            dve.wait_ge(ld_late, 32)
            mixed_q(0)
            mixed_v(0)

            def softmax_parts(i):
                for hh in range(2):
                    half = sc[:, 16 * hh:16 * hh + 16, :]
                    dve.wait_ge(score_psum, 2 * i + hh + 1)
                    dve.scalar_tensor_tensor(out=half, in0=slot[hh][:].rearrange("p (h k) -> p h k", h=16),
                                             scalar=HD ** -0.5, in1=tab_sb[:, 16 * hh:16 * hh + 16, :],
                                             op0=ALU.mult, op1=ALU.add).then_inc(score_ready, 1)
                    dve.wait_ge(score_ready, 2 * i + hh + 1)
                    dve.tensor_reduce(mx[:, 16 * hh:16 * hh + 16], half, AX.X, ALU.max).then_inc(max_ready, 1)
                for hh in range(2):
                    half = sc[:, 16 * hh:16 * hh + 16, :]
                    dve.wait_ge(exp_ready, 2 * i + hh + 1)
                    dve.tensor_reduce(sm[:, 16 * hh:16 * hh + 16], half, AX.X, ALU.add).then_inc(sum_ready, 1)
                    dve.wait_ge(sum_ready, 2 * i + hh + 1)
                    dve.reciprocal(rs[:, 16 * hh:16 * hh + 16], sm[:, 16 * hh:16 * hh + 16]).then_inc(rsum_ready, 1)

            def residual(n):
                dve.wait_ge(wo_psum, n + 1)
                dve.wait_ge(ld_xres, 16 * (n + 1))
                dve.tensor_tensor(xres[:], slot[1][:], xres[:], ALU.add).then_inc(x1_ready, 1)

            def at_low(i):
                dve.wait_ge(at_hi_ready, i + 1)
                split = "p c (b t) -> p b c t"
                dve.tensor_tensor(at_lo[:, :, :].rearrange(split, b=2),
                                  slot[2][:].rearrange("p (b c t) -> p b c t", b=2, c=KC),
                                  at_hi[:, :, :].bitcast(F32).rearrange(split, b=2), ALU.subtract
                                  ).then_inc(at_lo_ready, 1)

            softmax_parts(0)
            for c in range(KC):
                split_lo(KC + c, wo_hi, wo_lo, c)
            mixed_q(1)
            at_low(0)
            mixed_v(1)
            with dve.Fori(1, LAST - 1) as i:
                softmax_parts(i)
                mixed_q(i + 1)
                residual(i - 1)
                at_low(i)
                mixed_v(i + 1)
            softmax_parts(LAST - 1)
            mixed_q(LAST)
            dve.memset(x4[:, :, 0:1], 0.0)
            dve.memset(x4[:, :, LP + 1:LP + 2], 0.0).then_inc(pads_zero, 1)
            for c in range(4):
                split_lo(2 * KC + c, w_hi, w_lo, c)
            residual(LAST - 2)
            at_low(LAST - 1)
            mixed_v(LAST)
            softmax_parts(LAST)
            for c in range(4, KC):
                split_lo(2 * KC + c, w_hi, w_lo, c)
            residual(LAST - 1)
            at_low(LAST)

            def conv_sum(n, u):
                dve.wait_ge(conv_psum, n + 1)
                dve.wait_ge(ld_ctx, 16 * (n + 1))
                dve.tensor_tensor(cv[:, u, :, :], slot[0][:].rearrange("p (c t) -> p c t", c=KC),
                                  ctxb[:].unsqueeze(1).to_broadcast([P, KC, P]), ALU.add).then_inc(cv_ready, 1)

            def dense_sum(n):
                dve.wait_ge(main_psum, n + 1)
                dve.wait_ge(ld_x1r, 16 * (n + 1))
                dve.tensor_tensor(acc[:, bass.ds(n, 1), :], slot[1][:].unsqueeze(1), x1r[:].unsqueeze(1), ALU.add
                                  ).then_inc(acc_ready, 1)

            gb1, gamma, beta = (gc[:, GH * t:GH * t + GH] for t in range(3))
            gw2 = gc[:, 3 * GH:3 * GH + EX * GH].rearrange("p (e h) -> p e h", e=EX)
            gb2 = gc[:, 3 * GH + EX * GH:3 * GH + EX * GH + EX]
            rank = gc[:, 3 * GH + EX * GH + EX:3 * GH + EX * GH + 2 * EX]
            mean, var, std, rstd, gap, gap_e, top1, top2 = (g_s[:, t:t + 1] for t in range(8))

            def gate(n):
                steps = [0]

                def step(ins):
                    steps[0] += 1
                    ins.then_inc(gate_dve, 1)
                    dve.wait_ge(gate_dve, GATE_STEPS * n + steps[0])

                dve.wait_ge(lg_ready, n + 1)
                step(dve.tensor_tensor(g_h[:], g_in[:], gb1, ALU.add))
                step(dve.tensor_reduce(mean, g_h[:], AX.X, ALU.add))
                step(dve.tensor_scalar(mean, mean, 1.0 / GH, None, ALU.mult))
                step(dve.tensor_scalar(g_h[:], g_h[:], mean, None, ALU.subtract))
                step(dve.tensor_tensor(g_sq[:], g_h[:], g_h[:], ALU.mult))
                step(dve.tensor_reduce(var, g_sq[:], AX.X, ALU.add))
                step(dve.tensor_scalar(var, var, 1.0 / GH, 1e-5, ALU.mult, ALU.add))
                assert steps[0] == GATE_VAR
                dve.wait_ge(gate_act, 2 * n + 1)
                step(dve.reciprocal(rstd, std))
                step(dve.scalar_tensor_tensor(out=g_h[:], in0=g_h[:], scalar=rstd, in1=gamma, op0=ALU.mult, op1=ALU.mult))
                step(dve.tensor_tensor(g_h[:], g_h[:], beta, ALU.add))
                step(dve.tensor_scalar(g_h[:], g_h[:], 0.0, None, ALU.max))
                step(dve.tensor_tensor(g_prod[:], g_h[:].unsqueeze(1).to_broadcast([P, EX, GH]), gw2, ALU.mult))
                step(dve.tensor_reduce(gates[:], g_prod[:], AX.X, ALU.add))
                step(dve.tensor_tensor(gates[:], gates[:], gb2, ALU.add))
                for k, top in enumerate((top1, top2)):
                    step(dve.tensor_reduce(top, gates[:], AX.X, ALU.max))
                    step(dve.scalar_tensor_tensor(out=cand[:], in0=gates[:], scalar=top, in1=rank,
                                                  op0=ALU.is_equal, op1=ALU.mult))
                    step(dve.tensor_reduce(mean, cand[:], AX.X, ALU.max))
                    step(dve.tensor_scalar(hot1[:, k, :], cand[:], mean, None, ALU.is_equal))
                    if k == 0:
                        step(dve.scalar_tensor_tensor(out=gates[:], in0=hot1[:, 0, :], scalar=-3e38, in1=gates[:],
                                                      op0=ALU.mult, op1=ALU.add))
                step(dve.tensor_tensor(gap, top2, top1, ALU.subtract))
                assert steps[0] == GATE_GAP
                dve.wait_ge(gate_act, 2 * n + 2)
                step(dve.tensor_scalar(mean, gap_e, 1.0, None, ALU.add))
                step(dve.reciprocal(top1, mean))
                step(dve.tensor_scalar(top1, top1, 1.0 / R, None, ALU.mult))
                step(dve.tensor_tensor(top2, top1, gap_e, ALU.mult))
                dve.tensor_copy(hot[:, :, bass.ds(n, 1), :], hot1[:].unsqueeze(2))
                for k, top in enumerate((top1, top2)):
                    last = dve.tensor_scalar(whot[:, k, bass.ds(n, 1), :], hot1[:, k, :].unsqueeze(1), top, None, ALU.mult)
                step(last)
                assert steps[0] == GATE_STEPS

            conv_sum(0, 0)
            residual(LAST)
            conv_sum(1, 1)
            dve.wait_ge(ld_b, 32)
            gate(0)
            dense_sum(0)
            with dve.Fori(0, PAIRS // 2 - 1) as i:
                for u in range(2):
                    n = 2 * i + u + 1
                    dve.wait_ge(cv_lo_ready, n)
                    conv_sum(n + 1, u)
                    gate(n)
                    dense_sum(n)
            dve.memset(ones_c[:], 1.0)
            gate(LAST)
            for k in range(2):
                last = dve.tensor_reduce(cnt[:, k, :], hot[:, k, :, :].rearrange("p n e -> p e n"), AX.X, ALU.add)
            last.then_inc(cnt_hot, 1)
            dense_sum(LAST)
            dve.wait_ge(cnt_psum, 1)
            dve.tensor_scalar(allow[:], bank6[:, 256:256 + 2 * EX].rearrange("p (k e) -> p k e", k=2),
                              float(CAPACITY), None, ALU.is_le).then_inc(routed, 1)
            dve.wait_ge(routed, 1)
            dve.tensor_tensor(whot[:], whot[:], allow[:].unsqueeze(2).to_broadcast([P, 2, PAIRS, EX]), ALU.mult
                              ).then_inc(routed, 1)
            dve.wait_ge(routed, 2)
            dve.tensor_tensor(wmix[:], whot[:, 0, :, :], whot[:, 1, :, :], ALU.add).then_inc(wmix_ready, 1)

            with dve.Fori(0, PAIRS // 2) as i:
                for u in range(2):
                    n = 2 * i + u
                    dve.wait_ge(lb_psum, n + 1)
                    dve.tensor_tensor(acc[:, bass.ds(n, 1), :], slot[u][:].unsqueeze(1), acc[:, bass.ds(n, 1), :],
                                      ALU.add).then_inc(out_ready, 1)


def _phased(a):
    return a.reshape(*a.shape[:-1], LP, PH).swapaxes(-1, -2).reshape(a.shape)


def _layout(i):
    x = np.asarray(i["x"], np.float32)
    rows = x.reshape(PAIRS, P, L)
    a = {}
    a["xt"] = rows.reshape(PAIRS, P, KC, P).transpose(0, 3, 2, 1)
    a["xp"] = _phased(rows)
    a["emb_t"] = i["cond_128"].T
    a["c_w0"] = i["L0_cond_W0"]
    a["c_b0"] = i["L0_cond_b0"].reshape(P, 1)
    a["c_w1"] = i["L0_cond_W1"]
    a["c_b1"] = i["L0_cond_b1"].reshape(P, 1)
    a["c_w2"] = i["L0_cond_W2"]
    a["c_b2"] = np.tile(i["L0_cond_b2"], (BS, 1))
    a["c_w"] = i["L0_cond_weight"][..., 0].transpose(0, 2, 1).reshape(EX, CH * CH)
    a["c_bk"] = np.stack([i["L0_cond_bias_k"]] * 2, 1)
    wqkv = i["L0_attn_Wqkv"].reshape(KC, P, QKV)
    a["wq"] = wqkv[:, :, :L]
    a["wkv"] = wqkv[:, :, L:].transpose(1, 0, 2)
    a["wo"] = _phased(i["L0_attn_Wo"]).reshape(KC, P, L)
    slopes = ((2.0 ** -0.25) ** np.arange(1, NH + 1, dtype=np.float64)).astype(np.float32)
    q, k = np.arange(CH)[:, None, None], np.arange(CH)[None, None, :]
    tab = np.where(k <= q, slopes[None, :, None] * (k - q).astype(np.float32), np.float32(NEG))
    a["tab"] = np.concatenate([tab, tab]).astype(np.float32)
    a["ident_d"] = np.eye(P, dtype=np.float32)
    w = i["L0_cond2_weight"]
    cw = np.zeros((PH, 32, 2, 3, PH, 32), np.float32)
    for s in range(3):
        for qi in range(PH):
            for po in range(PH):
                t = 4 * (s - 1) + qi - po + TAPS // 2
                if 0 <= t < TAPS:
                    for g in range(4):
                        at = 16 * (g % 2)
                        cw[qi, at:at + 16, g // 2, s, po, at:at + 16] = w[16 * g:16 * g + 16, :, t].T
    a["conv_w"] = cw.reshape(P, 2, 3, P)
    a["cw_t"] = i["L0_cond2_c_weight"].T
    a["fside"] = i["fside_S_0"].reshape(1, CH)

    def in_rows(m):
        return m.reshape(2, P, PH, -1).transpose(1, 0, 2, 3).reshape(P, KC, -1)

    a["ffn_w"] = in_rows(_phased(i["L0_ffn_weight"].T)).transpose(1, 0, 2)
    lora_a = i["L0_ffn_lora_A"].transpose(1, 0, 2).reshape(L, EX * R)
    a["lg_w"] = in_rows(np.concatenate([lora_a, i["L0_ffn_gw1"].T], 1))
    a["lora_b"] = _phased(i["L0_ffn_lora_B"].reshape(EX * R, L))
    a["gate_c"] = np.tile(np.concatenate([i["L0_ffn_gb1"], i["L0_ffn_ln_gamma"], i["L0_ffn_ln_beta"],
                                          i["L0_ffn_gw2"].reshape(-1), i["L0_ffn_gb2"],
                                          np.arange(EX, 0, -1).astype(np.float32)]), (P, 1))
    return {k: np.ascontiguousarray(v) for k, v in a.items()}


def kernel(**inputs):
    import concourse.bacc as _bacc
    from concourse.bass_utils import run_bass_kernel_spmd as _run

    host = _layout({k: np.asarray(v) for k, v in inputs.items()})
    nc = _bacc.Bacc("TRN2", target_bir_lowering=False, num_devices=1)
    arrays, args = {}, {}
    for name, a in host.items():
        arrays[f"in_{name}"] = a
        args[name] = nc.dram_tensor(f"in_{name}", a.shape, mybir.dt.from_np(a.dtype), kind="ExternalInput").ap()
    out = nc.dram_tensor("out_0", (PAIRS, P, L), F32, kind="ExternalOutput").ap()
    build(nc, out=out, **args)
    r = _run(nc, [arrays], core_ids=[0]).results[0]["out_0"]
    return np.ascontiguousarray(r.reshape(BS * CH, PH, LP).swapaxes(1, 2)).reshape(BS, CH, L)
```

```python
from contextlib import ExitStack

import numpy as np

import concourse.bass as bass
from concourse import mybir

F32 = mybir.dt.float32
F32R = mybir.dt.float32r
ALU = mybir.AluOpType
ACT = mybir.ActivationFunctionType
AX = mybir.AxisListType

P = 128
BS, CH, L = 32, 64, 1024
PAIRS = BS // 2
KC = L // P
NH, HD = 32, 32
QKV = NH * HD + 2 * HD
EX = 8
R = 16
GH = 4 * EX
LG = EX * R + GH
TAPS, PH = 9, 8
LP = L // PH
GROUPS = 4
GC = CH // GROUPS
Y_CUT = 416
N_TOK = BS * CH
CAPACITY = int(3.0 * N_TOK / EX)
XC = PH * (LP + 1)
HALF = 1024
NEG = -1e30
COND1 = BS + 2 * (P + 1)
COND2 = 2 * EX + 4 * CH
COND_ATT = 4
COND_ROWS = 8
COND_AGG = 5
GP = 4
GATE_PARTS = (7, 15, 27, 32)


def wait_past(eng, semaphore, value):
    if not isinstance(value, int) or value > 0:
        eng.wait_ge(semaphore, value)


def build(nc, xt, xp, cond1_d, cond2_d, c_w, wq, wkv, wo, tab, ident_d, conv_w, ffn_w, lg_w, lora_b, gate_c, out):
    agg_d = nc.dram_tensor("agg_d", (BS, CH, CH), F32, kind="Internal").ap()
    aggb_d = nc.dram_tensor("aggb_d", (PAIRS, P), F32, kind="Internal").ap()
    ctxb_d = nc.dram_tensor("ctxb_d", (PAIRS, P), F32, kind="Internal").ap()
    x1_d = nc.dram_tensor("x1_d", (PAIRS, P, XC), F32, kind="Internal").ap()

    ctx = ExitStack()
    with ctx:
        def sb(name, shape, dt=F32, stack=ctx):
            return stack.enter_context(nc.sbuf_tensor(name, shape, dt))

        def sem(name):
            return ctx.enter_context(nc.semaphore(name))

        weights = ExitStack()
        wq_hi = sb("wq_hi", [P, KC, QKV], F32R, weights)
        wq_lo = sb("wq_lo", [P, KC, QKV], F32R, weights)
        weights.close()
        wd_hi = sb("wd_hi", [P, KC, L], F32R)
        wd_lo = sb("wd_lo", [P, KC, L], F32R)
        wc = sb("wc", [P, GROUPS, 2, P])
        assert 2 * QKV == 2 * L + P
        stage = sb("stage", [P, L])
        x8a = sb("x8a", [P, 2 * GROUPS, LP + 1])
        ident = sb("ident", [P, P])

        a_mem = ExitStack()
        early = ExitStack()
        cw_sb = sb("cw_sb", [EX, CH * CH], F32, early)
        agg_sb = sb("agg_sb", [P, L], F32, early)
        early.close()
        wo_hi = sb("wo_hi", [P, KC, L], F32R, a_mem)
        wo_lo = sb("wo_lo", [P, KC, L], F32R, a_mem)
        late = ExitStack()
        spare = sb("spare", [P, L], F32, late)
        late.close()
        x_hi = sb("x_hi", [P, KC, P], F32R, a_mem)
        x_lo = sb("x_lo", [P, KC, P], F32R, a_mem)
        tab_sb = sb("tab_sb", [P, NH, CH], F32, a_mem)
        qt = sb("qt", [P, KC, P], F32, a_mem)
        sc = sb("sc", [P, NH, CH], F32, a_mem)
        pt = sb("pt", [P, NH // 2, P], F32, a_mem)
        xt_sb = sb("xt_sb", [P, KC, P], F32, a_mem)
        y = sb("y", [P, L], F32, a_mem)
        bdk = sb("bdk", [P, 2, 4, CH], F32, a_mem)
        bdagg = sb("bdagg", [P, 2, 2, CH], F32, a_mem)
        bdv = sb("bdv", [P, 2, 2 * HD], F32, a_mem)
        aggb = sb("aggb", [P, P], F32, a_mem)
        yk4 = sb("yk4", [P, 4, HD], F32, a_mem)
        yv = sb("yv", [P, HD], F32, a_mem)
        ones = sb("ones", [P, P], F32, a_mem)
        cs_q = sb("cs_q", [P, KC + 1], F32, a_mem)
        cs_v = sb("cs_v", [P, HD], F32, a_mem)
        aggb_c = sb("aggb_c", [P, BS], F32, a_mem)
        aggb_p = sb("aggb_p", [P, 2], F32, a_mem)
        mx = sb("mx", [P, NH], F32, a_mem)
        sm = sb("sm", [P, NH], F32, a_mem)
        rs = sb("rs", [P, NH], F32, a_mem)
        warm = sb("warm", [P, 1], F32, a_mem)
        h_sb = sb("h_sb", [P, 2, BS], F32, a_mem)
        att = sb("att", [BS, EX], F32, a_mem)
        att_s = sb("att_s", [BS, 3], F32, a_mem)
        att_t = sb("att_t", [EX, BS], F32, a_mem)
        rows = sb("rows", [BS, 2, CH], F32, a_mem)
        early = ExitStack()
        wsum = sb("wsum", [P, QKV], F32, early)
        wsumk4 = sb("wsumk4", [P, 4, HD], F32, early)
        wkv_sb = sb("wkv_sb", [P, KC, 2 * HD], F32, early)
        cond1 = sb("cond1", [P, COND1], F32, early)
        cond2 = sb("cond2", [P, COND2], F32, early)
        emb_sb, w0_sb, b0_sb, w1_sb, b1_sb = (cond1[:, a:b] for a, b in (
            (0, BS), (BS, BS + P), (BS + P, BS + P + 1), (BS + P + 1, BS + 2 * P + 1), (BS + 2 * P + 1, COND1)))
        w2_sb, b2_sb = cond2[:, 0:EX], cond2[0:BS, EX:2 * EX]
        bk_sb = cond2[0:EX, 2 * EX:2 * EX + 2 * CH]
        cwt_sb, fs_sb = cond2[:, 2 * EX + 2 * CH:2 * EX + 3 * CH], cond2[0:1, 2 * EX + 3 * CH:COND2]
        early.close()
        early = ExitStack()
        spare2 = sb("spare2", [P, 2, L], F32, early)
        early.close()
        at_hi = sb("at_hi", [P, KC, P], F32R, a_mem)
        at_lo = sb("at_lo", [P, KC, P], F32R, a_mem)
        xres = sb("xres", [P, PH, LP + 1], F32, a_mem)
        a_mem.close()

        cv_all = sb("cv_all", [P, PAIRS, KC, P])
        ring = ExitStack()
        cv = sb("cv", [P, 2, KC, P], F32, ring)
        ring.close()
        x1r = sb("x1r", [P, 2, PH, LP + 1])
        lgw = sb("lgw", [P, KC, LG])
        ctxb = sb("ctxb", [P, 2, P])
        x8b = sb("x8b", [P, 2 * GROUPS, LP + 1])
        lg_all = sb("lg_all", [P, PAIRS, LG])
        lb_hi = sb("lb_hi", [P, L], F32R)
        lb_lo = sb("lb_lo", [P, L], F32R)
        cv_hi = sb("cv_hi", [P, 2, KC, P], F32R)
        cv_lo = sb("cv_lo", [P, 2, KC, P], F32R)
        gc = sb("gc", [P, 3 * GH + EX * GH + 2 * EX])
        g_h = sb("g_h", [P, GP, GH])
        g_sq = sb("g_sq", [P, GP, GH])
        g_prod = sb("g_prod", [P, GP, EX, GH])
        g_s = sb("g_s", [P, 8, GP])
        gates = sb("gates", [P, GP, EX])
        cand = sb("cand", [P, GP, EX])
        hot1 = sb("hot1", [P, 2, GP, EX])
        hot = sb("hot", [P, 2, PAIRS, EX])
        whot = sb("whot", [P, 2, PAIRS, EX])
        cnt = sb("cnt", [P, 2, EX])
        allow = sb("allow", [P, 2, EX])
        wmix = sb("wmix", [P, PAIRS, EX])
        ones_c = sb("ones_c", [P, P])
        tmpw = sb("tmpw", [P, 2, EX * R])
        tt_hi = sb("tt_hi", [P, 2, P], F32R)
        tt_lo = sb("tt_lo", [P, 2, P], F32R)

        rows3 = "p a b -> p (a b)"
        places = [stage[:], x8a[:].rearrange(rows3)[:, 0:L], sc[:, 0:16, :].rearrange(rows3), sc[:, 16:32, :].rearrange(rows3),
                  pt[:, 0:8, :].rearrange(rows3), pt[:, 8:16, :].rearrange(rows3), xres[:].rearrange(rows3)[:, 0:L],
                  xt_sb[:].rearrange(rows3), y[:], spare[:],
                  spare2[:, 0, :], spare2[:, 1, :]]
        PLACE = [0, 1, 2, 3, 4, 5, 0, 1] + [6, 0, 1, 10, 11, 6, 0, 1] + [0, 7, 9, 8, 0, 7, 9, 8]

        def before_in_place(n):
            return max((m for m in range(n) if PLACE[m] == PLACE[n]), default=None)

        def landed(eng, n):
            eng.wait_ge(ld_stage[PLACE[n]], 16 * (PLACE[:n + 1].count(PLACE[n])))

        slot = [ctx.enter_context(nc.psum_tensor(f"slot{i}", [P, HALF], F32)) for i in range(3)]
        bank6 = ctx.enter_context(nc.psum_tensor("bank6", [P, 512], F32))
        bank7 = ctx.enter_context(nc.psum_tensor("bank7", [P, 512], F32))

        ld_cond1, ld_cond2, ld_const = sem("ld_cond1"), sem("ld_cond2"), sem("ld_const")
        ld_cw, ld_wc, ld_tab = sem("ld_cw"), sem("ld_wc"), sem("ld_tab")
        ld_wkv = sem("ld_wkv")
        ld_stage = [sem(f"ld_stage{k}") for k in range(len(places))]
        ld_xt, ld_agg, ld_aggb, ld_xres = sem("ld_xt"), sem("ld_agg"), sem("ld_aggb"), sem("ld_xres")
        st_rows, st_x1 = sem("st_rows"), sem("st_x1")
        zeroed, cond_pe, cond_act, cond_dve = sem("zeroed"), sem("cond_pe"), sem("cond_act"), sem("cond_dve")
        agg_copied = sem("agg_copied")
        w_hi_done, w_lo_done, w_sum_done = sem("w_hi_done"), sem("w_lo_done"), sem("w_sum_done")
        wsum_kv, cs_psum, cs_ready = sem("wsum_kv"), sem("cs_psum"), sem("cs_ready")
        wkv_hi_done, wkv_lo_done, kv_ready = sem("wkv_hi_done"), sem("wkv_lo_done"), sem("kv_ready")
        x_hi_ready, x_lo_ready, y_psum, y_ready = sem("x_hi_ready"), sem("x_lo_ready"), sem("y_psum"), sem("y_ready")
        qt_psum, qt_part, qt_ready, vv_psum = sem("qt_psum"), sem("qt_part"), sem("qt_ready"), sem("vv_psum")
        aggb_picked, bdv_ready = sem("aggb_picked"), sem("bdv_ready")
        score_psum, score_ready, max_ready = sem("score_psum"), sem("score_ready"), sem("max_ready")
        shifted, exp_ready, sum_ready = sem("shifted"), sem("exp_ready"), sem("sum_ready")
        pt_psum, pt_ready = sem("pt_psum"), sem("pt_ready")
        rsum_ready, prob_ready = ([sem(f"{n}{hh}") for hh in range(2)] for n in ("rsum_ready", "prob_ready"))
        at_psum, at_hi_ready, at_lo_ready = sem("at_psum"), sem("at_hi_ready"), sem("at_lo_ready")
        wo_psum, x1_ready = sem("wo_psum"), sem("x1_ready")
        ld_lgw, ld_lb, ld_gc, st_out = sem("ld_lgw"), sem("ld_lb"), sem("ld_gc"), sem("st_out")
        ld_x8, ld_ctx, ld_x1r = ([sem(f"{n}{u}") for u in range(2)] for n in ("ld_x8", "ld_ctx", "ld_x1r"))
        conv_psum, cv_ready, cv_kept = sem("conv_psum"), sem("cv_ready"), sem("cv_kept")
        lg_psum, lg_ready = sem("lg_psum"), sem("lg_ready")
        gate_dve, gate_act = sem("gate_dve"), sem("gate_act")
        cnt_hot, cnt_psum, wmix_ready = sem("cnt_hot"), sem("cnt_psum"), sem("wmix_ready")
        routed, lb_hi_ready, lb_lo_ready = sem("routed"), sem("lb_hi_ready"), sem("lb_lo_ready")
        cv_hi_ready, cv_lo_ready, main_psum = sem("cv_hi_ready"), sem("cv_lo_ready"), sem("main_psum")
        tmpw_ready, tt_psum, tt_hi_ready, tt_lo_ready = sem("tmpw_ready"), sem("tt_psum"), sem("tt_hi_ready"), sem("tt_lo_ready")
        lora_half, lora_psum, out_half, out_ready = sem("lora_half"), sem("lora_psum"), sem("out_half"), sem("out_ready")

        LAST = PAIRS - 1
        flat = "p a b -> p (a b)"

        def in_blocks(t, h):
            return t[:, 4 * h:4 * h + 4, 1 - h:1 - h + LP]

        def product(s, h):
            return slot[s][:, 512 * h:512 * h + 512].rearrange("p (q k) -> p q k", q=PH // 2)

        block = ctx.enter_context(nc.Block())

        @block.sync
        def _(sp):
            sp.dma_start(cond1[:], cond1_d).then_inc(ld_cond1, 16)
            sp.dma_start(cond2[:], cond2_d).then_inc(ld_cond2, 16)
            sp.dma_start(ident[:], ident_d).then_inc(ld_const, 16)
            sp.dma_start(xt_sb[:], xt[0]).then_inc(ld_xt, 16)
            sp.dma_start(cw_sb[:], c_w).then_inc(ld_cw, 16)
            sp.dma_start(wkv_sb[:], wkv).then_inc(ld_wkv, 16)

            def stage_in(n, src):
                m = before_in_place(n)
                if m is not None:
                    sp.wait_ge(w_hi_done, m + 1)
                    sp.wait_ge(w_lo_done, m + 1)
                    if m < KC:
                        sp.wait_ge(w_sum_done, m + 1)
                sp.dma_start(places[PLACE[n]], src).then_inc(ld_stage[PLACE[n]], 16)

            for c in range(KC):
                stage_in(c, wq[c])
            sp.wait_ge(agg_copied, 1)
            for g in range(4):
                sp.dma_start(agg_d[:, GC * g:GC * g + GC, :].rearrange("b i o -> b (i o)"),
                             agg_sb[BS * g:BS * g + BS, :]).then_inc(st_rows, 16)
            sp.wait_ge(cond_dve, COND_ROWS)
            sp.dma_start(aggb_d.rearrange("n (b o) -> (n b) o", b=2), rows[:, 0, :]).then_inc(st_rows, 16)
            sp.dma_start(ctxb_d.rearrange("n (b o) -> (n b) o", b=2), rows[:, 1, :]).then_inc(st_rows, 16)
            sp.dma_start(tab_sb[:], tab).then_inc(ld_tab, 16)
            sp.wait_ge(st_rows, 96)
            sp.wait_ge(zeroed, 4)

            def load_agg(n):
                for b in range(2):
                    for r in range(2):
                        sp.dma_start(bdagg[CH * b:CH * b + CH, b, r, :], agg_d[2 * n + b]).then_inc(ld_agg, 16)
                sp.dma_start(aggb[:], aggb_d[n].partition_broadcast(P)).then_inc(ld_aggb, 16)

            load_agg(0)
            for c in range(2):
                stage_in(KC + c, wo[c])

            def next_x(n):
                sp.wait_ge(y_psum, n)
                sp.dma_start(xt_sb[:], xt[n]).then_inc(ld_xt, 16)

            def next_agg(n):
                sp.wait_ge(vv_psum, n)
                sp.wait_ge(qt_ready, n)
                load_agg(n)

            def residual(n):
                wait_past(sp, st_x1, 16 * n)
                sp.dma_start(xres[:].rearrange(flat), xp[n]).then_inc(ld_xres, 16)

            def store_x1(n):
                sp.wait_ge(x1_ready, n + 1)
                sp.dma_start(x1_d[n], xres[:].rearrange(flat)).then_inc(st_x1, 16)

            next_x(1)
            stage_in(KC + 2, wo[2])
            sp.wait_ge(cs_psum, 1)
            stage_in(KC + 3, wo[3])
            stage_in(KC + 4, wo[4])
            next_agg(1)
            for c in range(5, KC):
                stage_in(KC + c, wo[c])
            next_x(2)
            next_agg(2)
            sp.wait_ge(w_hi_done, 2 * KC)
            sp.wait_ge(w_lo_done, 2 * KC)
            residual(0)
            next_x(3)
            store_x1(0)

            def a_loads(i):
                next_agg(i + 1)
                residual(i - 1)
                next_x(i + 2)
                store_x1(i - 1)

            with sp.Fori(2, LAST - 1) as i:
                a_loads(i)

            next_agg(LAST)
            residual(LAST - 2)
            for c in range(4):
                if c == 1:
                    sp.wait_ge(y_psum, PAIRS)
                if c == 3:
                    sp.wait_ge(qt_psum, PAIRS)
                stage_in(2 * KC + c, ffn_w[c])
            store_x1(LAST - 2)
            residual(LAST - 1)

            def load_x8(n, u):
                sp.dma_start((x8a, x8b)[u][:], x1_d[n].rearrange("(g c) (q k) -> (c q) g k", c=GC, q=PH)
                             ).then_inc(ld_x8[u], 16)

            def load_conv(n, u):
                load_x8(n, u)
                load_ctx(n, u)

            def load_ctx(n, u):
                sp.dma_start(ctxb[:, u, :], ctxb_d[n].partition_broadcast(P)).then_inc(ld_ctx[u], 16)

            for c in range(4, KC):
                stage_in(2 * KC + c, ffn_w[c])
            sp.dma_start(wc[:], conv_w).then_inc(ld_wc, 16)
            load_x8(0, 0)
            sp.wait_ge(score_ready, 2 * PAIRS)
            load_ctx(0, 0)
            load_conv(1, 1)
            sp.dma_start(lgw[:], lg_w).then_inc(ld_lgw, 16)
            store_x1(LAST - 1)
            residual(LAST)
            sp.wait_ge(w_hi_done, 2 * KC + 5)
            sp.wait_ge(w_lo_done, 2 * KC + 5)
            sp.dma_start(stage[:], lora_b).then_inc(ld_lb, 16)
            sp.wait_ge(conv_psum, 1)
            sp.wait_ge(cv_ready, 1)
            load_conv(2, 0)
            sp.wait_ge(conv_psum, 2)
            sp.wait_ge(cv_ready, 2)
            load_conv(3, 1)
            store_x1(LAST)
            sp.dma_start(gc[:], gate_c).then_inc(ld_gc, 16)
            sp.wait_ge(st_x1, 16 * PAIRS)

            with sp.Fori(2, PAIRS // 2) as i:
                for u in range(2):
                    sp.wait_ge(conv_psum, 2 * i + u - 1)
                    sp.wait_ge(cv_ready, 2 * i + u - 1)
                    load_conv(2 * i + u, u)

            def load_x1r(n, u):
                sp.dma_start(x1r[:, u, :, :].rearrange(flat), x1_d[n]).then_inc(ld_x1r[u], 16)

            def store(n, u):
                sp.wait_ge(out_ready, n + 1)
                sp.dma_start(out[n], x1r[:, u, :, :].rearrange(flat)).then_inc(st_out, 16)

            sp.wait_ge(lg_psum, PAIRS)
            sp.wait_ge(cv_kept, PAIRS)
            load_x1r(0, 0)
            load_x1r(1, 1)
            with sp.Fori(0, PAIRS // 2 - 1) as i:
                for u in range(2):
                    store(2 * i + u, u)
                    sp.wait_ge(st_out, 16 * (2 * i + u + 1))
                    load_x1r(2 * i + u + 2, u)
            store(LAST - 1, 0)
            for h in range(2):
                sp.wait_ge((out_half, out_ready)[h], PAIRS)
                sp.dma_start(out[LAST].rearrange("p (h n) -> p h n", h=2)[:, h, :],
                             x1r[:, 1, 4 * h:4 * h + 4, :].rearrange(flat)).then_inc(st_out, 16)
            sp.wait_ge(st_out, 16 * (PAIRS + 1))

        @block.tensor
        def _(pe):
            def split_product(dst, a_hi, a_lo, b_hi, b_lo, before=lambda c: None, whole=True):
                for c in range(KC):
                    before(c)
                    for t, (a, b) in enumerate(((a_hi, b_hi), (a_hi, b_lo), (a_lo, b_hi))):
                        at = 0
                        for d in dst:
                            m = pe.matmul(d, a(c), b[:, c, at:at + d.shape[1]],
                                          start=(c == 0 and t == 0), stop=(whole and c == KC - 1 and t == 2))
                            at += d.shape[1]
                return m

            def banks(s):
                return [slot[s][:, 0:512], slot[s][:, 512:1024]]

            pe.wait_ge(ld_cond1, 16)
            pe.matmul(bank7[:, 0:BS], w0_sb, emb_sb, start=True, stop=True).then_inc(cond_pe, 1)
            pe.wait_ge(cond_act, 1)
            pe.matmul(bank7[:, BS:2 * BS], w1_sb, h_sb[:, 0, :], start=True, stop=True).then_inc(cond_pe, 1)
            pe.wait_ge(cond_act, 2)
            pe.wait_ge(ld_cond2, 16)
            pe.matmul(bank7[0:BS, 64:64 + EX], h_sb[:, 1, :], w2_sb, start=True, stop=True).then_inc(cond_pe, 1)
            pe.wait_ge(cond_dve, COND_ATT)
            pe.wait_ge(ld_const, 16)
            pe.transpose(bank7[0:EX, 128:128 + BS], att[:], ident[0:BS, 0:BS]).then_inc(cond_pe, 1)
            pe.wait_ge(cond_dve, COND_ATT + 1)
            pe.wait_ge(zeroed, 4)
            pe.matmul(bank7[0:BS, 192:192 + CH], att_t[:], bk_sb[:, 0:CH], start=True, stop=True)
            pe.matmul(bank7[:, 256:256 + BS], bk_sb, att_t[:], start=True, stop=True)
            pe.matmul(bank7[0:BS, 320:320 + CH], ones[0:1, 0:BS], fs_sb, start=True, stop=False)
            pe.matmul(bank7[0:BS, 320:320 + CH], emb_sb, cwt_sb, start=False, stop=True).then_inc(cond_pe, 1)
            pe.wait_ge(ld_cw, 16)
            for k in range(2):
                for g in range(4):
                    at = HALF * g + 512 * k
                    m = pe.matmul(slot[0][BS * g:BS * g + BS, 512 * k:512 * k + 512], att_t[:],
                                  cw_sb[:, at:at + 512], start=True, stop=True)
            m.then_inc(cond_pe, 1)

            def products(n, before=lambda c: None):
                pe.wait_ge(x_hi_ready, n + 1)
                pe.wait_ge(x_lo_ready, n + 1)
                split_product([slot[2][:, 0:Y_CUT], slot[2][:, 512:512 + Y_CUT], bank6[:, 0:QKV - 2 * Y_CUT]],
                              lambda c: x_hi[:, c, :], lambda c: x_lo[:, c, :], wq_hi, wq_lo, before
                              ).then_inc(y_psum, 1)

            def mix_q(n):
                pe.wait_ge(y_ready, n + 1)
                pe.wait_ge(ld_agg, 64 * (n + 1))
                for c in range(KC):
                    if c == 2 * Y_CUT // P:
                        pe.wait_ge(kv_ready, n + 1)
                    pe.matmul(slot[2][:, P * c:P * c + P].rearrange("p (b o) -> p b o", b=2),
                              y[:, P * c:P * c + P], bdagg[:, :, 0, :], start=True, stop=True)
                pe.matmul(bank6[:, 2 * P:3 * P].rearrange("p (b o) -> p b o", b=2), yk4[:, :, :].rearrange(flat),
                          bdagg[:, :, 0, :], start=True, stop=True).then_inc(qt_psum, 1)

            def mix_v(n):
                for b in range(2):
                    m = pe.matmul(bank7[:, HD * b:HD * b + HD], bdagg[:, b, :, :].rearrange(flat), yv[:],
                                  start=True, stop=True)
                m.then_inc(vv_psum, 1)

            def scores(i):
                for hh in range(2):
                    if hh == 1 and isinstance(i, int) and i == 1:
                        pe.wait_ge(at_lo_ready, 1)
                    for c in range(4):
                        if 4 * hh + c < KC - 1:
                            pe.wait_ge(qt_part, (KC - 1) * i + 4 * hh + c + 1)
                        else:
                            pe.wait_ge(qt_ready, i + 1)
                        for b in range(2):
                            m = pe.matmul(slot[hh][CH * b:CH * b + CH, 256 * c:256 * c + 256],
                                          qt[:, 4 * hh + c, CH * b:CH * b + CH],
                                          bdk[:, b, :, :].rearrange(flat), start=True, stop=True)
                    m.then_inc(score_psum, 1)

            def turn_probs(i):
                for hh in range(2):
                    pe.wait_ge(prob_ready[hh], i + 1)
                    for k in range(8):
                        h = 16 * hh + 2 * k
                        m = pe.transpose(slot[hh][:, P * k:P * k + P], sc[:, h:h + 2, :].rearrange(flat), ident[:])
                    m.then_inc(pt_psum, 1)

            def attend(i, s=2):
                pe.wait_ge(pt_ready, 2 * i + 2)
                pe.wait_ge(bdv_ready, i + 1)
                for b in range(2):
                    for eo in range(2):
                        m = pe.matmul(slot[s][CH * eo:CH * eo + CH, 512 * b:512 * b + 512]
                                      .rearrange("p (c t) -> p c t", c=KC), bdv[:, b, :],
                                      pt[:, eo::2, CH * b:CH * b + CH], start=True, stop=True)
                m.then_inc(at_psum, 1)

            def project(n, s=1):
                pe.wait_ge(at_hi_ready, n + 1)
                pe.wait_ge(at_lo_ready, n + 1)
                split_product(banks(s), lambda c: at_hi[:, c, :], lambda c: at_lo[:, c, :], wo_hi, wo_lo
                              ).then_inc(wo_psum, 1)

            def chunk_split(c):
                pe.wait_ge(w_hi_done, c + 1)
                pe.wait_ge(w_lo_done, c + 1)

            pe.wait_ge(wkv_hi_done, 1)
            pe.wait_ge(wkv_lo_done, 1)
            products(0, chunk_split)
            pe.wait_ge(wsum_kv, 2)
            pe.wait_ge(w_sum_done, KC)
            pe.wait_ge(cond_dve, COND_ROWS)
            for c in range(KC):
                pe.matmul(bank7[:, 128 + c:129 + c], wsum[:, P * c:P * c + P], ones[:, 0:1], start=True, stop=True)
            pe.matmul(bank7[:, 136:137], wsumk4[:, :, :].rearrange(flat), ones[:, 0:1], start=True, stop=True)
            pe.matmul(bank7[:, 160:160 + HD], ones[:], wsum[:, L + HD:QKV], start=True, stop=True
                      ).then_inc(cs_psum, 1)
            mix_q(0)
            pe.wait_ge(cs_ready, 2)
            mix_v(0)

            def pair(i):
                wait_past(pe, x1_ready, i - 1)
                scores(i)
                wait_past(pe, at_lo_ready, i)
                products(i + 1)
                turn_probs(i)
                mix_q(i + 1)
                if not isinstance(i, int) or i > 0:
                    pe.wait_ge(pt_ready, 2 * i + 2)
                    if isinstance(i, int):
                        chunk_split(2 * KC - 1)
                    project(i - 1)
                if isinstance(i, int) and i == 0:
                    attend(0, 1)
                else:
                    pe.wait_ge(qt_ready, i + 2)
                    attend(i)
                mix_v(i + 1)

            pe.wait_ge(agg_copied, 1)
            pair(0)
            pair(1)
            with pe.Fori(2, LAST) as i:
                pair(i)
            pe.wait_ge(x1_ready, LAST - 1)
            scores(LAST)
            project(LAST - 1, 2)

            turned = (bank6, bank7)

            def conv(i, u, dst):
                pe.wait_ge(ld_x8[u], 16 * (i + 1))
                for g in range(2 * GROUPS):
                    for s in range(2):
                        m = pe.matmul(dst[g], (x8a, x8b)[u][:, g, s:s + LP], wc[:, g % GROUPS, s, :],
                                      start=(s == 0), stop=(s == 1))
                m.then_inc(conv_psum, 1)

            def groups(t):
                return [t[:, P * g:P * g + P] for g in range(t.shape[1] // P)]

            def gate_and_lora(n, u):
                pe.wait_ge(cv_ready, n + 1)
                wait_past(pe, lg_ready, n - 1)
                for c in range(KC):
                    m = pe.matmul(turned[u][:, 0:LG], cv[:, u, c, :], lgw[:, c, :], start=(c == 0), stop=(c == KC - 1))
                m.then_inc(lg_psum, 1)

            pe.wait_ge(ld_wc, 16)
            pe.wait_ge(qt_ready, PAIRS)
            pe.wait_ge(bdv_ready, PAIRS)
            conv(0, 0, groups(bank6) + groups(bank7))
            turn_probs(LAST)
            pe.wait_ge(x1_ready, LAST)
            conv(0, 1, groups(slot[2]))
            attend(LAST, 0)
            pe.wait_ge(ld_lgw, 16)
            gate_and_lora(0, 0)
            project(LAST)

            def two_pairs(i, first=False):
                for u in range(2):
                    pe.wait_ge(cv_ready, 2 * i + u + 1)
                    conv(i + 1, u, groups(slot[2 * u]))
                    if not (first and u == 0):
                        gate_and_lora(2 * i + u, u)

            two_pairs(0, True)
            with pe.Fori(1, PAIRS // 2 - 1) as i:
                two_pairs(i)
            gate_and_lora(LAST - 1, 0)
            gate_and_lora(LAST, 1)

            def turn_weighted(n, u):
                pe.wait_ge(tmpw_ready, n + 1)
                wait_past(pe, tt_lo_ready, n - 1)
                pe.transpose(turned[u][:, 0:P], tmpw[:, u, :], ident[:]).then_inc(tt_psum, 1)

            def dense(n, u, s, before=lambda c: None):
                pe.wait_ge(cv_hi_ready, n + 1)
                pe.wait_ge(cv_lo_ready, n + 1)
                wait_past(pe, out_ready, n - 1)
                split_product(banks(s), lambda c: cv_hi[:, u, c, :], lambda c: cv_lo[:, u, c, :], wd_hi, wd_lo,
                              before, whole=False).then_inc(main_psum, 1)

            def lora(n, u, s):
                pe.wait_ge(tt_hi_ready, n + 1)
                pe.wait_ge(tt_lo_ready, n + 1)
                for k, d in enumerate(banks(s)):
                    for t, (a, b) in enumerate(((tt_hi, lb_hi), (tt_hi, lb_lo), (tt_lo, lb_hi))):
                        m = pe.matmul(d, a[:, u, :], b[:, 512 * k:512 * k + 512], start=False, stop=(t == 2))
                    m.then_inc((lora_half, lora_psum)[k], 1)

            chunk_split(3 * KC - 1)
            pe.wait_ge(lb_hi_ready, 1)
            pe.wait_ge(lb_lo_ready, 1)
            pe.wait_ge(x1_ready, PAIRS)
            dense(0, 0, 2)

            def routing(c):
                if c == 2:
                    pe.wait_ge(cnt_hot, 1)
                    pe.wait_ge(lg_ready, PAIRS)
                    pe.matmul(bank6[:, 256:256 + 2 * EX], ones_c[:], cnt[:, :, :].rearrange(flat),
                              start=True, stop=True).then_inc(cnt_psum, 1)
                if c in (6, 7):
                    turn_weighted(c - 6, c - 6)

            dense(1, 1, 1, routing)
            lora(0, 0, 2)
            lora(1, 1, 1)
            with pe.Fori(1, PAIRS // 2) as i:
                for u in range(2):
                    dense(2 * i + u, u, u, lambda c: turn_weighted(2 * i + u, u) if c == 5 else None)
                    lora(2 * i + u, u, u)

        @block.scalar
        def _(act):
            act.wait_ge(zeroed, 4)
            act.activation(warm[:], ones[:, 0:1], ACT.Gelu)
            act.wait_ge(ld_cond1, 16)
            for t in range(2):
                act.wait_ge(cond_pe, t + 1)
                act.activation(h_sb[:, t, :], bank7[:, BS * t:BS * t + BS], ACT.Gelu, bias=(b0_sb, b1_sb)[t]
                               ).then_inc(cond_act, 1)
            act.wait_ge(cond_dve, 2)
            act.activation(att[:], att[:], ACT.Exp, bias=att_s[:, 0:1], accum_out=att_s[:, 1:2]).then_inc(cond_act, 1)

            def split_hi(n, dst, c):
                landed(act, n)
                act.activation(dst[:, c, 0:L], places[PLACE[n]], ACT.Copy).then_inc(w_hi_done, 1)

            def x_high(n):
                act.wait_ge(ld_xt, 16 * (n + 1))
                act.activation(x_hi[:], xt_sb[:], ACT.Copy).then_inc(x_hi_ready, 1)

            def y_copy(n):
                act.wait_ge(y_psum, n + 1)
                act.activation(y[:, 0:2 * Y_CUT].rearrange("p (k n) -> p k n", k=2),
                               slot[2][:].rearrange("p (k n) -> p k n", k=2)[:, :, 0:Y_CUT], ACT.Copy
                               ).then_inc(y_ready, 1)
                k_at = L - 2 * Y_CUT
                act.activation(y[:, 2 * Y_CUT:L], bank6[:, 0:k_at], ACT.Copy)
                act.activation(yk4[:], bank6[:, k_at:k_at + HD].unsqueeze(1).to_broadcast([P, 4, HD]), ACT.Copy)
                act.activation(yv[:], bank6[:, k_at + HD:k_at + 2 * HD], ACT.Copy).then_inc(kv_ready, 1)

            def exps(i):
                for hh in range(2):
                    act.wait_ge(shifted, 2 * i + hh + 1)
                    half = sc[:, 16 * hh:16 * hh + 16, :]
                    act.activation(half, half, ACT.Exp).then_inc(exp_ready, 1)

            def pt_copy(i):
                for hh in range(2):
                    act.wait_ge(pt_psum, 2 * i + hh + 1)
                    act.activation(pt[:, 8 * hh:8 * hh + 8, :], slot[hh][:].rearrange("p (h t) -> p h t", h=8),
                                   ACT.Copy).then_inc(pt_ready, 1)

            def at_high(i, s=2):
                act.wait_ge(at_psum, i + 1)
                act.activation(at_hi[:, :, :].rearrange("p c (b t) -> p b c t", b=2),
                               slot[s][:].rearrange("p (b c t) -> p b c t", b=2, c=KC), ACT.Copy
                               ).then_inc(at_hi_ready, 1)

            x_high(0)
            act.wait_ge(ld_wkv, 16)
            act.activation(wq_hi[:, :, L:QKV], wkv_sb[:], ACT.Copy).then_inc(wkv_hi_done, 1)
            for c in range(3):
                split_hi(c, wq_hi, c)
            act.wait_ge(cond_pe, COND_AGG + 1)
            act.activation(agg_sb[:], slot[0][:], ACT.Copy).then_inc(agg_copied, 1)
            for c in range(3, KC):
                split_hi(c, wq_hi, c)
            y_copy(0)
            act.wait_ge(st_rows, 96)
            x_high(1)
            for c in range(5):
                split_hi(KC + c, wo_hi, c)
            exps(0)
            y_copy(1)
            pt_copy(0)
            act.wait_ge(w_lo_done, KC + 5)
            at_high(0, 1)
            x_high(2)

            def pair(i):
                exps(i)
                if isinstance(i, int):
                    for c in range(5, KC):
                        split_hi(KC + c, wo_hi, c)
                y_copy(i + 1)
                pt_copy(i)
                x_high(i + 2)
                at_high(i)

            pair(1)
            with act.Fori(2, LAST - 1) as i:
                pair(i)
            exps(LAST - 1)
            y_copy(LAST)
            pt_copy(LAST - 1)
            for c in range(4):
                split_hi(2 * KC + c, wd_hi, c)
            at_high(LAST - 1)
            exps(LAST)
            for c in range(4, KC):
                split_hi(2 * KC + c, wd_hi, c)
            pt_copy(LAST)
            at_high(LAST, 0)

            turned = (bank6, bank7)

            def keep(n, u):
                act.wait_ge(cv_ready, n + 1)
                act.activation(cv_all[:, bass.ds(n, 1), :, :], cv[:, u, :, :].unsqueeze(1), ACT.Copy).then_inc(cv_kept, 1)

            def lg_copy(n, u):
                act.wait_ge(lg_psum, n + 1)
                act.activation(lg_all[:, bass.ds(n, 1), :], turned[u][:, 0:LG].unsqueeze(1), ACT.Copy
                               ).then_inc(lg_ready, 1)

            def root(g):
                act.wait_ge(gate_dve, GATE_PARTS[3] * g + GATE_PARTS[0])
                act.activation(g_s[:, 2, :], g_s[:, 1, :], ACT.Sqrt).then_inc(gate_act, 1)

            def exp_gap(g):
                act.wait_ge(gate_dve, GATE_PARTS[3] * g + GATE_PARTS[2])
                act.activation(g_s[:, 5, :], g_s[:, 4, :], ACT.Exp).then_inc(gate_act, 1)

            def conv_high(n, u):
                wait_past(act, main_psum, n - 1)
                act.activation(cv_hi[:, u, :, :], cv_all[:, bass.ds(n, 1), :, :].rearrange("p a c t -> p (a c) t"),
                               ACT.Copy).then_inc(cv_hi_ready, 1)

            act.wait_ge(wo_psum, PAIRS)
            keep(0, 0)
            keep(1, 1)
            act.wait_ge(ld_lb, 16)
            act.activation(lb_hi[:], stage[:], ACT.Copy).then_inc(lb_hi_ready, 1)
            for n in range(GP):
                lg_copy(n, n % 2)
                keep(n + 2, n % 2)

            def group(g, last=False):
                root(g)
                for u in range(GP):
                    if u == 2:
                        exp_gap(g)
                    lg_copy(GP * g + GP + u, u % 2)
                    if not (last and u >= 2):
                        keep(GP * g + GP + 2 + u, u % 2)

            with act.Fori(0, PAIRS // GP - 2) as g:
                group(g)
            act.wait_ge(cv_kept, 2)
            conv_high(0, 0)
            conv_high(1, 1)
            group(PAIRS // GP - 2, True)
            root(PAIRS // GP - 1)
            exp_gap(PAIRS // GP - 1)

            def turned_high(n, u):
                act.wait_ge(tt_psum, n + 1)
                wait_past(act, lora_psum, n - 1)
                act.activation(tt_hi[:, u, :], turned[u][:, 0:P], ACT.Copy).then_inc(tt_hi_ready, 1)

            act.wait_ge(cv_kept, PAIRS)
            conv_high(2, 0)
            turned_high(0, 0)
            turned_high(1, 1)
            conv_high(3, 1)
            with act.Fori(1, PAIRS // 2 - 1) as i:
                for u in range(2):
                    turned_high(2 * i + u, u)
                    conv_high(2 * i + u + 2, u)
            turned_high(LAST - 1, 0)
            turned_high(LAST, 1)

        @block.gpsimd
        def _(pool):
            for t, v in ((bdagg, 0.0), (bdk, 0.0), (bdv, 0.0), (ones, 1.0)):
                pool.memset(t[:], v).then_inc(zeroed, 1)

            def x_low(n):
                pool.wait_ge(x_hi_ready, n + 1)
                pool.tensor_tensor(x_lo[:], xt_sb[:], x_hi[:].bitcast(F32), ALU.subtract).then_inc(x_lo_ready, 1)

            for c in range(1, KC - 1):
                landed(pool, c)
                if c == 1:
                    landed(pool, 0)
                    before = places[PLACE[0]]
                else:
                    pool.wait_ge(w_sum_done, c)
                    before = wsum[:, 0:L]
                pool.tensor_tensor(wsum[:, 0:L], before, places[PLACE[c]], ALU.add
                                   ).then_inc(w_sum_done, 2 if c == 1 else 1)
            pool.wait_ge(y_psum, 1)
            x_low(1)

            def shift_and_norm(i):
                for hh in range(2):
                    pool.wait_ge(max_ready, 2 * i + hh + 1)
                    half = sc[:, 16 * hh:16 * hh + 16, :]
                    pool.tensor_tensor(half, half, mx[:, 16 * hh:16 * hh + 16].unsqueeze(2)
                                       .to_broadcast([P, 16, CH]), ALU.subtract).then_inc(shifted, 1)
                pool.wait_ge(rsum_ready[0], i + 1)
                half = sc[:, 0:16, :]
                pool.tensor_tensor(half, half, rs[:, 0:16].unsqueeze(2).to_broadcast([P, 16, CH]), ALU.mult
                                   ).then_inc(prob_ready[0], 1)

            with pool.Fori(0, LAST - 1) as i:
                shift_and_norm(i)
                x_low(i + 2)
            shift_and_norm(LAST - 1)
            shift_and_norm(LAST)

            def conv_low(n, u):
                pool.wait_ge(cv_hi_ready, n + 1)
                pool.tensor_tensor(cv_lo[:, u, :, :], cv_all[:, bass.ds(n, 1), :, :].rearrange("p a c t -> p (a c) t"),
                                   cv_hi[:, u, :, :].bitcast(F32), ALU.subtract).then_inc(cv_lo_ready, 1)

            def weigh(n, u):
                wait_past(pool, tt_psum, n - 1)
                pool.tensor_tensor(tmpw[:, u, :].rearrange("p (a e r) -> p a e r", a=1, r=R),
                                   lg_all[:, bass.ds(n, 1), 0:EX * R].rearrange("p a (e r) -> p a e r", r=R),
                                   wmix[:, bass.ds(n, 1), :].unsqueeze(3).to_broadcast([P, 1, EX, R]), ALU.mult
                                   ).then_inc(tmpw_ready, 1)

            conv_low(0, 0)
            conv_low(1, 1)
            pool.wait_ge(wmix_ready, 1)
            pool.wait_ge(lg_ready, PAIRS)
            weigh(0, 0)
            weigh(1, 1)
            with pool.Fori(1, PAIRS // 2) as i:
                for u in range(2):
                    conv_low(2 * i + u, u)
                    weigh(2 * i + u, u)

        @block.vector
        def _(dve):
            def cond(ins, value):
                ins.then_inc(cond_dve, 1)
                dve.wait_ge(cond_dve, value)

            dve.wait_ge(cond_pe, 3)
            dve.wait_ge(ld_cond2, 16)
            cond(dve.tensor_tensor(att[:], bank7[0:BS, 64:64 + EX], b2_sb, ALU.add), 1)
            cond(dve.tensor_reduce(att_s[:, 0:1], att[:], AX.X, ALU.max, negate=True), 2)
            dve.wait_ge(cond_act, 3)
            cond(dve.reciprocal(att_s[:, 2:3], att_s[:, 1:2]), 3)
            cond(dve.tensor_scalar(att[:], att[:], att_s[:, 2:3], None, ALU.mult), COND_ATT)
            dve.wait_ge(cond_pe, 4)
            cond(dve.tensor_copy(att_t[:], bank7[0:EX, 128:128 + BS]), COND_ATT + 1)
            dve.wait_ge(x_hi_ready, 1)
            dve.tensor_tensor(x_lo[:], xt_sb[:], x_hi[:].bitcast(F32), ALU.subtract).then_inc(x_lo_ready, 1)
            dve.wait_ge(cond_pe, COND_AGG)
            dve.tensor_copy(rows[:, 0, :], bank7[0:BS, 192:192 + CH]).then_inc(cond_dve, 1)
            dve.tensor_copy(rows[:, 1, :], bank7[0:BS, 320:320 + CH]).then_inc(cond_dve, 1)
            dve.tensor_copy(aggb_c[:], bank7[:, 256:256 + BS]).then_inc(cond_dve, 1)

            def split_lo(n, dst_hi, dst_lo, c):
                dve.wait_ge(w_hi_done, n + 1)
                dve.tensor_tensor(dst_lo[:, c, 0:L], places[PLACE[n]], dst_hi[:, c, 0:L].bitcast(F32), ALU.subtract
                                  ).then_inc(w_lo_done, 1)

            dve.wait_ge(wkv_hi_done, 1)
            dve.tensor_tensor(wq_lo[:, :, L:QKV], wkv_sb[:], wq_hi[:, :, L:QKV].bitcast(F32), ALU.subtract
                              ).then_inc(wkv_lo_done, 1)
            split_lo(0, wq_hi, wq_lo, 0)
            split_lo(1, wq_hi, wq_lo, 1)
            for c in range(2, KC):
                split_lo(c, wq_hi, wq_lo, c)
            dve.tensor_reduce(wsum[:, L:QKV], wkv_sb[:].rearrange("p c n -> p n c"), AX.X, ALU.add).then_inc(wsum_kv, 1)
            dve.wait_ge(wsum_kv, 1)
            dve.wait_ge(w_sum_done, KC - 1)
            dve.tensor_tensor(wsum[:, 0:L], wsum[:, 0:L], places[PLACE[KC - 1]], ALU.add).then_inc(w_sum_done, 1)
            dve.tensor_copy(wsumk4[:], wsum[:, L:L + HD].unsqueeze(1).to_broadcast([P, 4, HD])).then_inc(wsum_kv, 1)
            dve.wait_ge(cs_psum, 1)
            dve.tensor_copy(cs_q[:], bank7[:, 128:128 + KC + 1]).then_inc(cs_ready, 1)
            dve.tensor_copy(cs_v[:], bank7[:, 160:160 + HD]).then_inc(cs_ready, 1)
            dve.wait_ge(cs_ready, 2)

            def mixed_q(n):
                dve.wait_ge(qt_psum, n + 1)
                dve.wait_ge(ld_aggb, 16 * (n + 1))
                for j in range(4):
                    q = slice(32 * j, 32 * j + 32)
                    dve.scalar_tensor_tensor(
                        out=bdk[q, :, j, :], in0=aggb[q, :].rearrange("p (b k) -> p b k", b=2),
                        scalar=cs_q[q, KC:KC + 1], in1=bank6[q, 2 * P:3 * P].rearrange("p (b k) -> p b k", b=2),
                        op0=ALU.mult, op1=ALU.add)
                for c in range(KC):
                    dve.scalar_tensor_tensor(out=qt[:, c, :], in0=aggb[:], scalar=cs_q[:, c:c + 1],
                                             in1=slot[2][:, P * c:P * c + P], op0=ALU.mult, op1=ALU.add
                                             ).then_inc(qt_part if c < KC - 1 else qt_ready, 1)

            def mixed_v(n):
                dve.wait_ge(vv_psum, n + 1)
                dve.tensor_copy(aggb_p[:], aggb_c[:, bass.ds(2 * n, 2)]).then_inc(aggb_picked, 1)
                dve.wait_ge(aggb_picked, n + 1)
                for b in range(2):
                    for r in range(2):
                        q = slice(CH * r, CH * r + CH)
                        last = dve.scalar_tensor_tensor(
                            out=bdv[q, b, HD * r:HD * r + HD], in0=cs_v[q, :], scalar=aggb_p[q, b:b + 1],
                            in1=bank7[q, HD * b:HD * b + HD], op0=ALU.mult, op1=ALU.add)
                last.then_inc(bdv_ready, 1)

            dve.wait_ge(zeroed, 4)
            dve.wait_ge(cond_dve, COND_ROWS)
            mixed_q(0)
            mixed_v(0)
            dve.wait_ge(ld_tab, 16)

            def softmax_parts(i):
                for hh in range(2):
                    half = sc[:, 16 * hh:16 * hh + 16, :]
                    dve.wait_ge(score_psum, 2 * i + hh + 1)
                    dve.scalar_tensor_tensor(out=half, in0=slot[hh][:].rearrange("p (h k) -> p h k", h=16),
                                             scalar=HD ** -0.5, in1=tab_sb[:, 16 * hh:16 * hh + 16, :],
                                             op0=ALU.mult, op1=ALU.add).then_inc(score_ready, 1)
                    dve.wait_ge(score_ready, 2 * i + hh + 1)
                    dve.tensor_reduce(mx[:, 16 * hh:16 * hh + 16], half, AX.X, ALU.max).then_inc(max_ready, 1)
                for hh in range(2):
                    half = sc[:, 16 * hh:16 * hh + 16, :]
                    dve.wait_ge(exp_ready, 2 * i + hh + 1)
                    dve.tensor_reduce(sm[:, 16 * hh:16 * hh + 16], half, AX.X, ALU.add).then_inc(sum_ready, 1)
                    dve.wait_ge(sum_ready, 2 * i + hh + 1)
                    dve.reciprocal(rs[:, 16 * hh:16 * hh + 16], sm[:, 16 * hh:16 * hh + 16]).then_inc(rsum_ready[hh], 1)
                dve.wait_ge(rsum_ready[1], i + 1)
                dve.tensor_tensor(half, half, rs[:, 16:32].unsqueeze(2).to_broadcast([P, 16, CH]), ALU.mult
                                  ).then_inc(prob_ready[1], 1)

            def residual(n, s=1):
                dve.wait_ge(wo_psum, n + 1)
                dve.wait_ge(ld_xres, 16 * (n + 1))
                for h in range(2):
                    m = dve.tensor_tensor(in_blocks(xres, h), product(s, h), in_blocks(xres, h), ALU.add)
                m.then_inc(x1_ready, 1)

            def at_low(i, s=2):
                dve.wait_ge(at_hi_ready, i + 1)
                split = "p c (b t) -> p b c t"
                dve.tensor_tensor(at_lo[:, :, :].rearrange(split, b=2),
                                  slot[s][:].rearrange("p (b c t) -> p b c t", b=2, c=KC),
                                  at_hi[:, :, :].bitcast(F32).rearrange(split, b=2), ALU.subtract
                                  ).then_inc(at_lo_ready, 1)

            softmax_parts(0)
            for c in range(5):
                split_lo(KC + c, wo_hi, wo_lo, c)
            mixed_q(1)
            at_low(0, 1)
            softmax_parts(1)
            mixed_v(1)
            for c in range(5, KC):
                split_lo(KC + c, wo_hi, wo_lo, c)
            mixed_q(2)
            residual(0)
            at_low(1)
            with dve.Fori(2, LAST - 1) as i:
                softmax_parts(i)
                mixed_v(i)
                mixed_q(i + 1)
                residual(i - 1)
                at_low(i)
            softmax_parts(LAST - 1)
            mixed_v(LAST - 1)
            mixed_q(LAST)
            for c in range(4):
                split_lo(2 * KC + c, wd_hi, wd_lo, c)
            residual(LAST - 2)
            at_low(LAST - 1)
            mixed_v(LAST)
            softmax_parts(LAST)
            for c in range(4, KC):
                split_lo(2 * KC + c, wd_hi, wd_lo, c)
                if c == 5:
                    residual(LAST - 1, 2)

            def conv_sum(n, u, parts=None):
                dve.wait_ge(conv_psum, n + 1)
                dve.wait_ge(ld_ctx[u], 16 * (n // 2 + 1))
                wait_past(dve, cv_kept, n - 1)
                wait_past(dve, lg_psum, n - 1)
                for k, t in enumerate(parts):
                    w = t.shape[1] // PH
                    m = dve.tensor_tensor(cv[:, u, :, w * k:w * k + w].rearrange("p c (g t) -> p c g t", t=GC),
                                          t.rearrange("p (g c t) -> p c g t", c=PH, t=GC),
                                          ctxb[:, u, w * k:w * k + w].rearrange("p (c g t) -> p c g t", c=1, t=GC)
                                          .to_broadcast([P, KC, w // GC, GC]), ALU.add)
                m.then_inc(cv_ready, 1)

            gb1, gamma, beta = (gc[:, GH * t:GH * t + GH].unsqueeze(1).to_broadcast([P, GP, GH]) for t in range(3))
            at = 3 * GH
            gw2 = gc[:, at:at + EX * GH].rearrange("p (a e h) -> p a e h", a=1, e=EX).to_broadcast([P, GP, EX, GH])
            at += EX * GH
            gb2 = gc[:, at:at + EX].unsqueeze(1).to_broadcast([P, GP, EX])
            rank = gc[:, at + EX:at + 2 * EX].unsqueeze(1).to_broadcast([P, GP, EX])
            mean, var, std, rstd, gap, gap_e, top1, top2 = (g_s[:, t, :] for t in range(8))

            def by(v, n):
                return v.unsqueeze(2).to_broadcast([P, GP, n])

            def gate(g, part):
                steps = [(0, *GATE_PARTS)[part]]

                def step(ins):
                    steps[0] += 1
                    ins.then_inc(gate_dve, 1)
                    dve.wait_ge(gate_dve, GATE_PARTS[3] * g + steps[0])

                tt = dve.tensor_tensor
                if part == 0:
                    dve.wait_ge(lg_ready, GP * g + GP)
                    step(tt(g_h[:], lg_all[:, bass.ds(GP * g, GP), EX * R:LG], gb1, ALU.add))
                    step(dve.tensor_reduce(mean, g_h[:], AX.X, ALU.add))
                    step(dve.tensor_scalar(mean, mean, 1.0 / GH, None, ALU.mult))
                    step(tt(g_h[:], g_h[:], by(mean, GH), ALU.subtract))
                    step(tt(g_sq[:], g_h[:], g_h[:], ALU.mult))
                    step(dve.tensor_reduce(var, g_sq[:], AX.X, ALU.add))
                    step(dve.tensor_scalar(var, var, 1.0 / GH, 1e-5, ALU.mult, ALU.add))
                if part == 1:
                    dve.wait_ge(gate_act, 2 * g + 1)
                    step(dve.reciprocal(rstd, std))
                    step(tt(g_h[:], g_h[:], by(rstd, GH), ALU.mult))
                    step(tt(g_h[:], g_h[:], gamma, ALU.mult))
                    step(tt(g_h[:], g_h[:], beta, ALU.add))
                    step(dve.tensor_scalar(g_h[:], g_h[:], 0.0, None, ALU.max))
                    step(tt(g_prod[:], g_h[:].unsqueeze(2).to_broadcast([P, GP, EX, GH]), gw2, ALU.mult))
                    step(dve.tensor_reduce(gates[:], g_prod[:], AX.X, ALU.add))
                    step(tt(gates[:], gates[:], gb2, ALU.add))
                if part == 2:
                    for k, top in enumerate((top1, top2)):
                        step(dve.tensor_reduce(top, gates[:], AX.X, ALU.max))
                        step(tt(cand[:], gates[:], by(top, EX), ALU.is_equal))
                        step(tt(cand[:], cand[:], rank, ALU.mult))
                        step(dve.tensor_reduce(mean, cand[:], AX.X, ALU.max))
                        step(tt(hot1[:, k, :, :], cand[:], by(mean, EX), ALU.is_equal))
                        if k == 0:
                            step(dve.scalar_tensor_tensor(out=gates[:], in0=hot1[:, 0, :, :], scalar=-3e38, in1=gates[:],
                                                          op0=ALU.mult, op1=ALU.add))
                    step(tt(gap, top2, top1, ALU.subtract))
                if part == 3:
                    dve.wait_ge(gate_act, 2 * g + 2)
                    step(dve.tensor_scalar(mean, gap_e, 1.0, None, ALU.add))
                    step(dve.reciprocal(top1, mean))
                    step(dve.tensor_scalar(top1, top1, 1.0 / R, None, ALU.mult))
                    step(tt(top2, top1, gap_e, ALU.mult))
                    dve.tensor_copy(hot[:, :, bass.ds(GP * g, GP), :], hot1[:])
                    for k, top in enumerate((top1, top2)):
                        last = tt(whot[:, k, bass.ds(GP * g, GP), :], hot1[:, k, :, :], by(top, EX), ALU.mult)
                    step(last)
                assert steps[0] == GATE_PARTS[part], steps

            dve.wait_ge(w_lo_done, 3 * KC)
            conv_sum(0, 0, (bank6[:], bank7[:]))
            conv_sum(1, 1, (slot[2][:],))
            at_low(LAST, 0)
            residual(LAST)
            evens, odds = (slot[0][:],), (slot[2][:],)
            for n in range(2, 6):
                conv_sum(n, n % 2, (evens, odds)[n % 2])
                if n == 2:
                    dve.wait_ge(lb_hi_ready, 1)
                    dve.tensor_tensor(lb_lo[:], stage[:], lb_hi[:].bitcast(F32), ALU.subtract).then_inc(lb_lo_ready, 1)
            dve.wait_ge(ld_gc, 16)

            def group(g, last=False):
                for part in range(4):
                    gate(g, part)
                    if not (last and part >= 2):
                        conv_sum(GP * g + GP + 2 + part, part % 2, (evens, odds)[part % 2])

            with dve.Fori(0, PAIRS // GP - 2) as g:
                group(g)
            group(PAIRS // GP - 2, True)
            dve.memset(ones_c[:], 1.0)
            for part in range(4):
                gate(PAIRS // GP - 1, part)

            for k in range(2):
                last = dve.tensor_reduce(cnt[:, k, :], hot[:, k, :, :].rearrange("p n e -> p e n"), AX.X, ALU.add)
            last.then_inc(cnt_hot, 1)
            dve.wait_ge(cnt_psum, 1)
            dve.tensor_scalar(allow[:], bank6[:, 256:256 + 2 * EX].rearrange("p (k e) -> p k e", k=2),
                              float(CAPACITY), None, ALU.is_le).then_inc(routed, 1)
            dve.wait_ge(routed, 1)
            dve.tensor_tensor(whot[:], whot[:], allow[:].unsqueeze(2).to_broadcast([P, 2, PAIRS, EX]), ALU.mult
                              ).then_inc(routed, 1)
            dve.wait_ge(routed, 2)
            dve.tensor_tensor(wmix[:], whot[:, 0, :, :], whot[:, 1, :, :], ALU.add).then_inc(wmix_ready, 1)

            def turned_low(n, u):
                dve.wait_ge(tt_hi_ready, n + 1)
                dve.tensor_tensor(tt_lo[:, u, :], (bank6, bank7)[u][:, 0:P], tt_hi[:, u, :].bitcast(F32), ALU.subtract
                                  ).then_inc(tt_lo_ready, 1)

            def out_sum(i, u, s):
                dve.wait_ge(ld_x1r[u], 16 * (i + 1))
                for h in range(2):
                    dve.wait_ge((lora_half, lora_psum)[h], 2 * i + u + 1)
                    t = in_blocks(x1r[:, u, :, :], h)
                    dve.tensor_tensor(t, product(s, h), t, ALU.add).then_inc((out_half, out_ready)[h], 1)

            turned_low(0, 0)
            turned_low(1, 1)
            out_sum(0, 0, 2)
            out_sum(0, 1, 1)
            with dve.Fori(1, PAIRS // 2) as i:
                for u in range(2):
                    turned_low(2 * i + u, u)
                    out_sum(i, u, u)


def _phased(a):
    return a.reshape(*a.shape[:-1], LP, PH).swapaxes(-1, -2).reshape(a.shape)


def _blocked(a):
    p = _phased(a)
    return np.roll(p.reshape(*a.shape[:-1], PH, LP), PH // 2, -2).reshape(a.shape)


def _layout(i):
    x = np.asarray(i["x"], np.float32)
    rows = x.reshape(PAIRS, P, L)
    a = {}
    a["xt"] = rows.reshape(PAIRS, P, KC, P).transpose(0, 3, 2, 1)
    xp = np.zeros((PAIRS, P, PH, LP + 1), np.float32)
    blocked = _blocked(rows).reshape(PAIRS, P, PH, LP)
    xp[:, :, :PH // 2, 1:], xp[:, :, PH // 2:, :LP] = blocked[:, :, :PH // 2], blocked[:, :, PH // 2:]
    a["xp"] = xp.reshape(PAIRS, P, XC)
    emb_t = i["cond_128"].T
    a["cond1_d"] = np.concatenate([emb_t, i["L0_cond_W0"], i["L0_cond_b0"].reshape(P, 1),
                                   i["L0_cond_W1"], i["L0_cond_b1"].reshape(P, 1)], 1)
    rest = (i["L0_cond_W2"], np.tile(i["L0_cond_b2"], (BS, 1)), i["L0_cond_bias_k"], i["L0_cond_bias_k"],
            i["L0_cond2_c_weight"].T, i["fside_S_0"].reshape(1, CH))
    a["cond2_d"] = np.concatenate([np.pad(m, ((0, P - m.shape[0]), (0, 0))) for m in rest], 1)
    a["c_w"] = i["L0_cond_weight"][..., 0].transpose(0, 2, 1).reshape(EX, CH * CH)
    wqkv = i["L0_attn_Wqkv"].reshape(KC, P, QKV)
    a["wq"] = wqkv[:, :, :L]
    a["wkv"] = wqkv[:, :, L:].transpose(1, 0, 2)
    a["wo"] = _blocked(i["L0_attn_Wo"]).reshape(KC, P, L)
    slopes = ((2.0 ** -0.25) ** np.arange(1, NH + 1, dtype=np.float64)).astype(np.float32)
    q, k = np.arange(CH)[:, None, None], np.arange(CH)[None, None, :]
    tab = np.where(k <= q, slopes[None, :, None] * (k - q).astype(np.float32), np.float32(NEG))
    a["tab"] = np.concatenate([tab, tab]).astype(np.float32)
    a["ident_d"] = np.eye(P, dtype=np.float32)
    w = i["L0_cond2_weight"]
    cw = np.zeros((GC, PH, GROUPS, 2, PH, GC), np.float32)
    for s in range(2):
        for qi in range(PH):
            for po in range(PH):
                t = PH * s + qi - po
                if 0 <= t < TAPS:
                    for g in range(GROUPS):
                        cw[:, qi, g, s, po, :] = w[GC * g:GC * g + GC, :, t].T
    a["conv_w"] = cw.reshape(P, GROUPS, 2, P)

    def in_rows(m):
        return m.reshape(LP, PH, -1)

    a["ffn_w"] = in_rows(_blocked(i["L0_ffn_weight"].T)).transpose(1, 0, 2)
    lora_a = i["L0_ffn_lora_A"].transpose(1, 0, 2).reshape(L, EX * R)
    a["lg_w"] = in_rows(np.concatenate([lora_a, i["L0_ffn_gw1"].T], 1))
    a["lora_b"] = _blocked(i["L0_ffn_lora_B"].reshape(EX * R, L))
    a["gate_c"] = np.tile(np.concatenate([i["L0_ffn_gb1"], i["L0_ffn_ln_gamma"], i["L0_ffn_ln_beta"],
                                          i["L0_ffn_gw2"].reshape(-1), i["L0_ffn_gb2"],
                                          np.arange(EX, 0, -1).astype(np.float32)]), (P, 1))
    return {k: np.ascontiguousarray(v) for k, v in a.items()}


def kernel(**inputs):
    import concourse.bacc as _bacc
    from concourse.bass_utils import run_bass_kernel_spmd as _run

    host = _layout({k: np.asarray(v) for k, v in inputs.items()})
    nc = _bacc.Bacc("TRN2", target_bir_lowering=False, num_devices=1)
    arrays, args = {}, {}
    for name, a in host.items():
        arrays[f"in_{name}"] = a
        args[name] = nc.dram_tensor(f"in_{name}", a.shape, mybir.dt.from_np(a.dtype), kind="ExternalInput").ap()
    out = nc.dram_tensor("out_0", (PAIRS, P, XC), F32, kind="ExternalOutput").ap()
    build(nc, out=out, **args)
    r = _run(nc, [arrays], core_ids=[0]).results[0]["out_0"]
    r = r.reshape(BS * CH, PH, LP + 1).swapaxes(1, 2).reshape(BS * CH, XC)
    return np.ascontiguousarray(r[:, PH // 2:PH // 2 + L]).reshape(BS, CH, L)
```
